# Optimizing a Trainium2 kernel written in Bass

```python
import numpy as np
import jax
import jax.numpy as jnp

def _softmax(x, axis=-1):
    return jax.nn.softmax(x, axis=axis)

def _gelu(x):
    return jax.nn.gelu(x, approximate=True)

def _silu(x):
    return jax.nn.silu(x)

def _sigmoid(x):
    return jax.nn.sigmoid(x)

def _layernorm(x, axis=-1, eps=1e-05):
    m = jnp.mean(x, axis=axis, keepdims=True)
    v = jnp.var(x, axis=axis, keepdims=True)
    return (x - m) / jnp.sqrt(v + eps)

def _scatter_add(tgt, idx, src, axis=0):
    return tgt.at[idx].add(src)

def _segment_sum(src, seg, n):
    return jax.ops.segment_sum(src, seg, n)
kernel_name = 'mk_macaron_d1_jaxref_r8_087d8a'

def setup_inputs(seed: int=0):
    np.random.seed(seed)
    _w = jnp.asarray

    def _L0_attn_setup():
        import jax, jax.numpy as jnp
        import numpy as np
        NUM_BLOCKS = 8
        D = 128
        FF = 512
        B, S = (4, 512)
        EPS_ATTN = 1e-06
        EPS_LN = 1e-06

        def _ln(x, scale, bias):
            m = jnp.mean(x, axis=-1, keepdims=True)
            v = jnp.var(x, axis=-1, keepdims=True)
            return (x - m) * jax.lax.rsqrt(v + EPS_LN) * scale + bias

        def _forward(x, Wq, bq, Wk, bk, Wv, bv, Wo, bo, ln1_s, ln1_b, W1, b1, W2, b2, ln2_s, ln2_b):
            gelu = lambda t: jax.nn.gelu(t, approximate=True)
            fmap = lambda t: jax.nn.elu(t) + 1.0
            for i in range(NUM_BLOCKS):
                residual = x
                Q = fmap(x @ Wq[i] + bq[i])
                K = fmap(x @ Wk[i] + bk[i])
                value = x @ Wv[i] + bv[i]
                KV = jnp.einsum('nsh,nsh->nh', K, value)
                Ksum = jnp.sum(K, axis=1)
                Z = 1.0 / (Q * Ksum[:, None, :] + EPS_ATTN)
                V = Q * KV[:, None, :] * Z
                attn_out = gelu(V @ Wo[i] + bo[i])
                x = _ln(attn_out + residual, ln1_s[i], ln1_b[i])
                residual = x
                h = gelu(x @ W1[i] + b1[i])
                ff_out = gelu(h @ W2[i] + b2[i])
                x = _ln(ff_out + residual, ln2_s[i], ln2_b[i])
            return x
        key = jax.random.key(seed)
        ks = jax.random.split(key, 16)
        g = lambda k, shape, fan: jax.random.normal(k, shape, jnp.float32) * (1.0 / np.sqrt(fan))
        inp = {'x': jax.random.normal(ks[0], (B, S, D), jnp.float32), 'Wq': g(ks[1], (NUM_BLOCKS, D, D), D), 'bq': jnp.zeros((NUM_BLOCKS, D), jnp.float32), 'Wk': g(ks[2], (NUM_BLOCKS, D, D), D), 'bk': jnp.zeros((NUM_BLOCKS, D), jnp.float32), 'Wv': g(ks[3], (NUM_BLOCKS, D, D), D), 'bv': jnp.zeros((NUM_BLOCKS, D), jnp.float32), 'Wo': g(ks[4], (NUM_BLOCKS, D, D), D), 'bo': jnp.zeros((NUM_BLOCKS, D), jnp.float32), 'ln1_s': jnp.ones((NUM_BLOCKS, D), jnp.float32), 'ln1_b': jnp.zeros((NUM_BLOCKS, D), jnp.float32), 'W1': g(ks[5], (NUM_BLOCKS, D, FF), D), 'b1': jnp.zeros((NUM_BLOCKS, FF), jnp.float32), 'W2': g(ks[6], (NUM_BLOCKS, FF, D), FF), 'b2': jnp.zeros((NUM_BLOCKS, D), jnp.float32), 'ln2_s': jnp.ones((NUM_BLOCKS, D), jnp.float32), 'ln2_b': jnp.zeros((NUM_BLOCKS, D), jnp.float32)}
        return inp
    _L0_attn_in = _L0_attn_setup()

    def _L0_ffn_setup():
        import jax, jax.numpy as jnp
        import numpy as np
        EPS = 1e-08

        def _ternary_linear(x, w):
            alpha = jnp.mean(jnp.abs(w))
            w_t = jnp.sign(w) * (jnp.abs(w) > 0.5 * alpha).astype(w.dtype)
            w_q = w + jax.lax.stop_gradient(w_t - w)
            d = x.shape[-1]
            rms = jnp.sqrt(jnp.sum(x * x, axis=-1, keepdims=True)) / jnp.sqrt(jnp.asarray(d, x.dtype))
            x_norm = x / (rms + EPS)
            return jnp.einsum('bsd,fd->bsf', x_norm, w_q)
        key = jax.random.key(seed)
        k1, k2, k3 = jax.random.split(key, 3)
        d_model, d_ff = (128, 512)
        B, S = (4, 512)
        x = jax.random.normal(k1, (B, S, d_model), dtype=jnp.float32)
        w_up = jax.random.normal(k2, (d_ff, d_model), dtype=jnp.float32) * 0.02
        w_down = jax.random.normal(k3, (d_model, d_ff), dtype=jnp.float32) * 0.02
        return {'x': x, 'w_up': w_up, 'w_down': w_down}
    _L0_ffn_in = _L0_ffn_setup()
    _d = {'L0_attn_x': _L0_attn_in['x'], 'L0_attn_Wq': _L0_attn_in['Wq'], 'L0_attn_bq': _L0_attn_in['bq'], 'L0_attn_Wk': _L0_attn_in['Wk'], 'L0_attn_bk': _L0_attn_in['bk'], 'L0_attn_Wv': _L0_attn_in['Wv'], 'L0_attn_bv': _L0_attn_in['bv'], 'L0_attn_Wo': _L0_attn_in['Wo'], 'L0_attn_bo': _L0_attn_in['bo'], 'L0_attn_ln1_s': _L0_attn_in['ln1_s'], 'L0_attn_ln1_b': _L0_attn_in['ln1_b'], 'L0_attn_W1': _L0_attn_in['W1'], 'L0_attn_b1': _L0_attn_in['b1'], 'L0_attn_W2': _L0_attn_in['W2'], 'L0_attn_b2': _L0_attn_in['b2'], 'L0_attn_ln2_s': _L0_attn_in['ln2_s'], 'L0_attn_ln2_b': _L0_attn_in['ln2_b'], 'L0_ffn_w_up': _L0_ffn_in['w_up'], 'L0_ffn_w_down': _L0_ffn_in['w_down']}
    _x0 = _d['L0_attn_x']
    _d['L0_attn_x'] = jax.random.normal(jax.random.fold_in(jax.random.key(seed), 1), (16, 256, 128), dtype=_x0.dtype)
    del _x0
    return _d

def reference(L0_attn_x, L0_attn_Wq, L0_attn_bq, L0_attn_Wk, L0_attn_bk, L0_attn_Wv, L0_attn_bv, L0_attn_Wo, L0_attn_bo, L0_attn_ln1_s, L0_attn_ln1_b, L0_attn_W1, L0_attn_b1, L0_attn_W2, L0_attn_b2, L0_attn_ln2_s, L0_attn_ln2_b, L0_ffn_w_up, L0_ffn_w_down):

    def _L0_attn_ref(x, Wq, bq, Wk, bk, Wv, bv, Wo, bo, ln1_s, ln1_b, W1, b1, W2, b2, ln2_s, ln2_b):
        import jax, jax.numpy as jnp
        import numpy as np
        NUM_BLOCKS = 8
        D = 128
        FF = 512
        B, S = (4, 512)
        EPS_ATTN = 1e-06
        EPS_LN = 1e-06

        def _ln(x, scale, bias):
            m = jnp.mean(x, axis=-1, keepdims=True)
            v = jnp.var(x, axis=-1, keepdims=True)
            return (x - m) * jax.lax.rsqrt(v + EPS_LN) * scale + bias

        def _forward(x, Wq, bq, Wk, bk, Wv, bv, Wo, bo, ln1_s, ln1_b, W1, b1, W2, b2, ln2_s, ln2_b):
            gelu = lambda t: jax.nn.gelu(t, approximate=True)
            fmap = lambda t: jax.nn.elu(t) + 1.0
            for i in range(NUM_BLOCKS):
                residual = x
                Q = fmap(x @ Wq[i] + bq[i])
                K = fmap(x @ Wk[i] + bk[i])
                value = x @ Wv[i] + bv[i]
                KV = jnp.einsum('nsh,nsh->nh', K, value)
                Ksum = jnp.sum(K, axis=1)
                Z = 1.0 / (Q * Ksum[:, None, :] + EPS_ATTN)
                V = Q * KV[:, None, :] * Z
                attn_out = gelu(V @ Wo[i] + bo[i])
                x = _ln(attn_out + residual, ln1_s[i], ln1_b[i])
                residual = x
                h = gelu(x @ W1[i] + b1[i])
                ff_out = gelu(h @ W2[i] + b2[i])
                x = _ln(ff_out + residual, ln2_s[i], ln2_b[i])
            return x
        return _forward(x, Wq, bq, Wk, bk, Wv, bv, Wo, bo, ln1_s, ln1_b, W1, b1, W2, b2, ln2_s, ln2_b)

    def _L0_ffn_ref(x, w_up, w_down):
        import jax, jax.numpy as jnp
        import numpy as np
        EPS = 1e-08

        def _ternary_linear(x, w):
            alpha = jnp.mean(jnp.abs(w))
            w_t = jnp.sign(w) * (jnp.abs(w) > 0.5 * alpha).astype(w.dtype)
            w_q = w + jax.lax.stop_gradient(w_t - w)
            d = x.shape[-1]
            rms = jnp.sqrt(jnp.sum(x * x, axis=-1, keepdims=True)) / jnp.sqrt(jnp.asarray(d, x.dtype))
            x_norm = x / (rms + EPS)
            return jnp.einsum('bsd,fd->bsf', x_norm, w_q)
        h = jax.nn.gelu(_ternary_linear(x, w_up), approximate=False)
        return _ternary_linear(h, w_down)
    x = L0_attn_x
    x = x + 0.5 * _L0_ffn_ref(_layernorm(x, axis=-1), L0_ffn_w_up, L0_ffn_w_down)
    x = x + _L0_attn_ref(_layernorm(x, axis=-1), L0_attn_Wq, L0_attn_bq, L0_attn_Wk, L0_attn_bk, L0_attn_Wv, L0_attn_bv, L0_attn_Wo, L0_attn_bo, L0_attn_ln1_s, L0_attn_ln1_b, L0_attn_W1, L0_attn_b1, L0_attn_W2, L0_attn_b2, L0_attn_ln2_s, L0_attn_ln2_b)
    x = x + 0.5 * _L0_ffn_ref(_layernorm(x, axis=-1), L0_ffn_w_up, L0_ffn_w_down)
    return x

_drawn_inputs = setup_inputs


def setup_inputs(seed=0):
    import zlib

    import numpy as np

    out = dict(_drawn_inputs(seed))
    spreads = {'L0_attn_bq': (0.0, 2.0),
     'L0_attn_bk': (0.0, 2.0),
     'L0_attn_bv': (0.0, 0.44),
     'L0_attn_bo': (0.0, 0.389),
     'L0_attn_ln1_s': (1.0, 0.2),
     'L0_attn_ln1_b': (0.0, 0.317),
     'L0_attn_b1': (0.0, 0.8),
     'L0_attn_b2': (0.0, 0.362),
     'L0_attn_ln2_s': (1.0, 0.2),
     'L0_attn_ln2_b': (0.0, 0.409)}
    factors = {'L0_attn_Wq': 29.368, 'L0_attn_Wk': 24.198}
    for name, (base, spread) in spreads.items():
        noise = np.random.default_rng([zlib.crc32(name.encode()), seed]).standard_normal(out[name].shape)
        drawn = base * np.exp(spread * noise) if base else spread * noise
        out[name] = jnp.asarray(drawn.astype(out[name].dtype))
    for name, factor in factors.items():
        out[name] = (out[name] * factor).astype(out[name].dtype)
    return out
```

```python
from contextlib import ExitStack

import concourse.bass as bass
from concourse import mybir

P = 128
LAYERS = 8
SEQ = 256
TILE = 2 * SEQ
NT = 8
BLK = TILE // P
FC = 4
FF = FC * P
TICKS = NT // 2

EPS_ATTN = 1e-6
EPS_LN = 1e-6
EPS_OUTER = 1e-5
EPS_RMS = 1e-8

F32 = mybir.dt.float32
F32R = mybir.dt.float32r
ALU = mybir.AluOpType
ACT = mybir.ActivationFunctionType
AX_X = mybir.AxisListType.X

BQ, BK, BV, BO, LN1S, LN1B, B2, LN2S, LN2B, B1 = (LAYERS * k for k in range(10))
NPAR = B1 + FC * LAYERS
DMA = 16


class Shared:
    pass


class Tile:

    def __init__(self, lay, rel):
        self.n = lay * NT + (rel + 1)
        self.layer = lay + rel // NT
        self.slot = rel % NT
        self.par = rel % 2
        self.chunks = lay * (NT * FC) + rel * FC
        self.first = rel % NT == 0


def tick_tiles(lay, tick):
    def tiles(*rels):
        if isinstance(lay, int):
            rels = [r for r in rels if 0 <= lay * NT + r < LAYERS * NT]
        return [Tile(lay, r) for r in rels]
    a = 2 * tick
    return tiles(a, a + 1), tiles(a - 2, a - 1), tiles(a - 4, a - 3), tiles(a - 5)


def at_least(eng, sem, value):
    if not isinstance(value, int) or value > 0:
        eng.wait_ge(sem, value)


def wait_apart(eng, s, sem, value):
    if not isinstance(value, int):
        value = eng.to_reg(value)
        eng.wait_ge(s.consts, 1)
    eng.wait_ge(sem, value)


def column(m, base, layer, k=0, per=1):
    if isinstance(layer, int):
        c = base + layer * per + k
        return m.par[:, c:c + 1]
    return m.par[:, bass.ds(layer * per + (base + k), 1)]


def macaron(nc, x_in, Wq, bq, Wk, bk, Wv, bv, Wo, bo, ln1_s, ln1_b, W1, b1, W2, b2, ln2_s, ln2_b,
            w_up, w_down, ident_in, out):
    x_rows = x_in.rearrange("b s d -> (b s) d").rearrange("(t j p) d -> t p j d", j=BLK, p=P)
    out_rows = out.rearrange("b s d -> (b s) d").rearrange("(t j p) d -> t p j d", j=BLK, p=P)
    W2_rows = W2.rearrange("l (c p) d -> l p c d", p=P)

    with ExitStack() as ctx:
        m, s = Shared(), Shared()

        def sb(name, shape, dt=F32):
            return ctx.enter_context(nc.sbuf_tensor(name, [P] + shape, dt))

        def sem(name):
            return ctx.enter_context(nc.semaphore(name))

        bank = [ctx.enter_context(nc.psum_tensor(f"bank{i}", [P, TILE], F32)) for i in range(8)]
        m.ps_q, m.ps_k, m.ps_v, m.ps_o, m.ps_h0, m.ps_h1, m.ps_ty, m.ps_tz = bank
        m.ps_h = (m.ps_h0, m.ps_h1)

        m.ident = sb("ident", [P])
        m.ones = sb("ones", [P])
        m.eps = sb("eps", [1])
        m.minus_half = sb("minus_half", [BLK])
        m.plus_half = sb("plus_half", [BLK])
        m.x_tm = sb("x_tm", [NT, BLK, P])
        m.x_fm = sb("x_fm", [NT, TILE])
        m.x_hi = sb("x_hi", [NT, TILE], F32R)
        m.x_lo = sb("x_lo", [NT, TILE], F32R)
        m.par_rows = sb("par_rows", [P])
        m.par = sb("par", [NPAR])
        m.upT = sb("upT", [FC, P], F32R)
        m.downT = sb("downT", [FC, P])
        m.wqkv = [sb(f"wqkv_{x}", [3, P], F32R) for x in ("hi", "lo")]
        m.w1 = [sb(f"w1_{x}", [FC, P], F32R) for x in ("hi", "lo")]
        m.wo = sb("wo", [P])
        m.w2 = sb("w2", [FC, P])
        m.next_qkv = [sb(f"next_qkv_{x}", [3, P], F32R) for x in ("hi", "lo")]
        m.next_w1 = [sb(f"next_w1_{x}", [FC, P], F32R) for x in ("hi", "lo")]
        m.raw_qkv = sb("raw_qkv", [3, P])
        m.raw_w1 = sb("raw_w1", [FC, P])

        m.e_k = sb("e_k", [2, TILE])
        m.e_q = sb("e_q", [2, TILE])
        m.elu_k = sb("elu_k", [2, TILE])
        m.elu_q = sb("elu_q", [2, TILE])
        m.kf = sb("kf", [2, TILE])
        m.kvf = sb("kvf", [2, TILE])
        m.ksum = sb("ksum", [2, 2])
        m.kvacc = sb("kvacc", [2, 2])
        m.kv = sb("kv", [2, 2])
        m.den = sb("den", [2, TILE])
        m.num = sb("num", [2, TILE])
        m.rec = sb("rec", [2, TILE])
        m.nwt = sb("nwt", [2, TILE])
        m.vf = sb("vf", [2, TILE])
        m.y = [sb(f"y{i}", [2, TILE]) for i in (1, 2)]
        m.z = [sb(f"z{i}", [2, BLK, P]) for i in (1, 2)]
        m.st = [sb(f"st{i}", [2, BLK, 6]) for i in (1, 2)]
        m.mv = [sb(f"mv{i}", [2, BLK, 2]) for i in (1, 2)]
        m.ve = [sb(f"ve{i}", [2, BLK]) for i in (1, 2)]
        m.rstd = [sb(f"rstd{i}", [2, BLK]) for i in (1, 2)]
        m.h = sb("h", [2, FC, TILE])

        s.setup_loaded = sem("setup_loaded")
        s.consts = sem("consts")
        s.abs_sums = sem("abs_sums")
        s.abs_total = sem("abs_total")
        s.thresholds = sem("thresholds")
        s.above = sem("above")
        s.ternary = sem("ternary")
        s.ternary_turned = sem("ternary_turned")
        s.par_turned = sem("par_turned")
        s.setup_kept = sem("setup_kept")
        s.raw_qkv_loaded = sem("raw_qkv_loaded")
        s.raw_w1_loaded = sem("raw_w1_loaded")
        s.wqkv_loaded = sem("wqkv_loaded")
        s.wo_loaded = sem("wo_loaded")
        s.w1_loaded = sem("w1_loaded")
        s.w2_loaded = sem("w2_loaded")
        s.raw_qkv_hi = sem("raw_qkv_hi")
        s.raw_w1_hi = sem("raw_w1_hi")
        s.next_qkv_split = sem("next_qkv_split")
        s.next_w1_split = sem("next_w1_split")
        s.proj_k = sem("proj_k")
        s.proj_q = sem("proj_q")
        s.proj_v = sem("proj_v")
        s.proj_o = sem("proj_o")
        s.ff_up = sem("ff_up")
        s.ff_down = sem("ff_down")
        s.turned_y1 = sem("turned_y1")
        s.turned_z1 = sem("turned_z1")
        s.turned_y2 = sem("turned_y2")
        s.turned_z2 = sem("turned_z2")
        s.exp_k = sem("exp_k")
        s.exp_q = sem("exp_q")
        s.ksum = sem("ksum")
        s.log_den = sem("log_den")
        s.recip = sem("recip")
        s.gelu_o = sem("gelu_o")
        s.gelu_h = sem("gelu_h")
        s.gelu_ff = sem("gelu_ff")
        s.x1_full = sem("x1_full")
        s.x_full = sem("x_full")
        s.neg_k = sem("neg_k")
        s.neg_q = sem("neg_q")
        s.expm1_k = sem("expm1_k")
        s.expm1_q = sem("expm1_q")
        s.elu_k = sem("elu_k")
        s.elu_q = sem("elu_q")
        s.kv_acc = sem("kv_acc")
        s.kv_ready = sem("kv_ready")
        s.newton_a = sem("newton_a")
        s.newton_c = sem("newton_c")
        s.v_ready = sem("v_ready")
        s.stats1 = sem("stats1")
        s.mv1 = sem("mv1")
        s.z1 = sem("z1")
        s.x1_hi = sem("x1_hi")
        s.stats2 = sem("stats2")
        s.mv2 = sem("mv2")
        s.z2 = sem("z2")
        s.x_hi = sem("x_hi")
        s.den_ready = sem("den_ready")
        s.num_ready = sem("num_ready")
        s.y1 = sem("y1")
        s.y2 = sem("y2")
        s.ve1 = sem("ve1")
        s.ve2 = sem("ve2")
        s.rstd1 = sem("rstd1")
        s.rstd2 = sem("rstd2")
        s.x1_split = sem("x1_split")
        s.x_split = sem("x_split")

        f = [ffn_buffers(sb, sem, m, tag) for tag in ("in", "out")]
        d = Shared()
        d.x_rows, d.out_rows, d.ident, d.w_up, d.w_down = x_rows, out_rows, ident_in, w_up, w_down
        d.qkv, d.Wo, d.W1, d.W2, d.b1 = (Wq, Wk, Wv), Wo, W1, W2_rows, b1
        d.vectors = ((BQ, bq), (BK, bk), (BV, bv), (BO, bo), (LN1S, ln1_s), (LN1B, ln1_b), (B2, b2),
                     (LN2S, ln2_s), (LN2B, ln2_b))

        block = ctx.enter_context(nc.Block())

        @block.sync
        def _(sp):
            sync_engine(sp, m, s, f, d)

        @block.tensor
        def _(pe):
            tensor_engine(pe, m, s, f)

        @block.scalar
        def _(act):
            scalar_engine(act, m, s, f)

        @block.vector
        def _(dve):
            vector_engine(dve, m, s, f)

        @block.gpsimd
        def _(pool):
            gpsimd_engine(pool, m, s, f)


def ffn_buffers(sb, sem, m, tag):
    f = Shared()
    f.first = tag == "in"
    if f.first:
        m.zc = [sb(f"zc_{x}", [2, TILE], F32R) for x in ("hi", "lo")]
        m.hsq = sb("hsq", [2, FC, TILE])
        m.hss = sb("hss", [2, TILE])
        m.scale = sb("scale", [2, 8, BLK])
        m.fz = sb("fz", [2, BLK, P])
        m.fst = sb("fst", [2, BLK, 6])
        m.fmv = sb("fmv", [2, BLK, 2])
        m.raw_tern, m.tern, m.below = m.hsq[:, 1, 0:2, :], m.hsq[:, 0, 0:2, :], m.hsq[:, 0, 2:4, :]
        m.abs_row = sb("abs_row", [2])
        m.thr = sb("thr", [2, 2])
    f.loaded = sem(f"ffn_{tag}_loaded")
    f.stored = sem(f"ffn_{tag}_stored")
    f.turned_x = sem(f"ffn_{tag}_turned_x")
    f.x_in = sem(f"ffn_{tag}_x_in")
    f.stats = sem(f"ffn_{tag}_stats")
    f.mv = sem(f"ffn_{tag}_mv")
    f.var_eps = sem(f"ffn_{tag}_var_eps")
    f.rstd = sem(f"ffn_{tag}_rstd")
    f.sd = sem(f"ffn_{tag}_sd")
    f.sd_rstd = sem(f"ffn_{tag}_sd_rstd")
    f.den = sem(f"ffn_{tag}_den")
    f.recip = sem(f"ffn_{tag}_recip")
    f.alpha = sem(f"ffn_{tag}_alpha")
    f.z = sem(f"ffn_{tag}_z")
    f.turned_z = sem(f"ffn_{tag}_turned_z")
    f.z_hi = sem(f"ffn_{tag}_z_hi")
    f.z_lo = sem(f"ffn_{tag}_z_lo")
    f.up = sem(f"ffn_{tag}_up")
    f.gelu = sem(f"ffn_{tag}_gelu")
    f.hsq = sem(f"ffn_{tag}_hsq")
    f.hss = sem(f"ffn_{tag}_hss")
    f.ssq = sem(f"ffn_{tag}_ssq")
    f.down = sem(f"ffn_{tag}_down")
    f.ms = sem(f"ffn_{tag}_ms")
    f.rms = sem(f"ffn_{tag}_rms")
    f.rms_eps = sem(f"ffn_{tag}_rms_eps")
    f.rms_recip = sem(f"ffn_{tag}_rms_recip")
    f.beta = sem(f"ffn_{tag}_beta")
    f.x_new = sem(f"ffn_{tag}_x_new")
    f.stats_c = sem(f"ffn_{tag}_stats_c")
    f.mv_c = sem(f"ffn_{tag}_mv_c")
    f.ve_c = sem(f"ffn_{tag}_ve_c")
    f.rstd_c = sem(f"ffn_{tag}_rstd_c")
    f.z_c = sem(f"ffn_{tag}_z_c")
    f.turned_c = sem(f"ffn_{tag}_turned_c")
    return f



def sync_engine(sp, m, s, f, d):
    fin, fout = f
    sp.dma_start(m.ident[:, :], d.ident).then_inc(s.setup_loaded, DMA)
    sp.dma_start(m.x_tm[:, 0, :, :], d.x_rows[0]).then_inc(fin.loaded, DMA)
    sp.dma_start(m.raw_tern[:, 0, :].rearrange("p (c d) -> p c d", c=FC),
                 d.w_up.rearrange("(c p) d -> p c d", p=P)).then_inc(s.setup_loaded, DMA)
    sp.dma_start(m.raw_tern[:, 1, :], d.w_down).then_inc(s.setup_loaded, DMA)
    for t in range(1, NT):
        sp.dma_start(m.x_tm[:, t, :, :], d.x_rows[t]).then_inc(fin.loaded, DMA)
    for base, v in d.vectors:
        sp.dma_start(m.par_rows[base:base + LAYERS, :], v).then_inc(s.setup_loaded, DMA)
    sp.dma_start(m.par_rows[B1:NPAR, :], d.b1.rearrange("l (c p) -> (l c) p", p=P)).then_inc(s.setup_loaded, DMA)

    def load_raw(lay):
        for i, w in enumerate(d.qkv):
            sp.dma_start(m.raw_qkv[:, i, :], w[lay]).then_inc(s.raw_qkv_loaded, DMA)
        sp.dma_start(m.raw_w1[:, :, :].rearrange("p c d -> p (c d)"), d.W1[lay]).then_inc(s.raw_w1_loaded, DMA)

    def switch_qkv(lay):
        wait_apart(sp, s, s.next_qkv_split, lay + 1)
        if not isinstance(lay, int):
            wait_apart(sp, s, s.proj_v, lay * NT)
        for i in range(2):
            sp.dma_start(m.wqkv[i][:, :, :].bitcast(F32), m.next_qkv[i][:, :, :].bitcast(F32)).then_inc(s.wqkv_loaded, DMA)

    def switch_wo(lay, src):
        if not isinstance(lay, int):
            wait_apart(sp, s, s.proj_o, lay * NT)
        sp.dma_start(m.wo[:, :], src).then_inc(s.wo_loaded, DMA)

    def switch_ff(lay, src):
        wait_apart(sp, s, s.next_w1_split, lay + 1)
        if not isinstance(lay, int):
            wait_apart(sp, s, s.ff_down, lay * NT)
        for i in range(2):
            sp.dma_start(m.w1[i][:, :, :].bitcast(F32), m.next_w1[i][:, :, :].bitcast(F32)).then_inc(s.w1_loaded, DMA)
        sp.dma_start(m.w2[:, :, :], src).then_inc(s.w2_loaded, DMA)

    load_raw(0)
    switch_qkv(0)
    switch_wo(0, d.Wo[0])
    switch_ff(0, d.W2[0])
    with sp.Fori(1, LAYERS) as lay:
        row = bass.ds(lay, 1)
        for i, w in enumerate(d.qkv):
            sp.dma_start(m.raw_qkv[:, i, :], w[row].rearrange("l p d -> p (l d)")).then_inc(s.raw_qkv_loaded, DMA)
        sp.dma_start(m.raw_w1[:, :, :].rearrange("p c d -> p (c d)"),
                     d.W1[row].rearrange("l p d -> p (l d)")).then_inc(s.raw_w1_loaded, DMA)
        switch_qkv(lay)
        switch_wo(lay, d.Wo[row].rearrange("l p d -> p (l d)"))
        switch_ff(lay, d.W2[row].rearrange("l p c d -> p (l c) d"))
    with sp.Fori(0, NT) as t:
        wait_apart(sp, s, fout.x_new, t + 1)
        sp.dma_start(d.out_rows[bass.ds(t, 1)].rearrange("t p j d -> p (t j) d"),
                     m.x_tm[:, bass.ds(t, 1), :, :].rearrange("p t j d -> p (t j) d")).then_inc(fout.stored, DMA)
    sp.wait_ge(fout.stored, DMA * NT)



def transpose_tile(pe, bank, src, m):
    for j in range(BLK):
        last = pe.transpose(bank[:, j * P:(j + 1) * P], src(j), m.ident[:, :])
    return last


def split_product(pe, bank, w_hi, w_lo, x_hi, x_lo):
    pe.matmul(bank[:, :], w_hi, x_hi, start=True, stop=False)
    pe.matmul(bank[:, :], w_hi, x_lo, start=False, stop=False)
    return pe.matmul(bank[:, :], w_lo, x_hi, start=False, stop=True)


def tensor_engine(pe, m, s, f):
    pe.wait_ge(s.setup_loaded, DMA * 13)
    pe.transpose(m.ps_q[:, 0:NPAR], m.par_rows[0:NPAR, :], m.ident[0:NPAR, 0:NPAR]).then_inc(s.par_turned, 1)
    pe.wait_ge(s.consts, 1)
    pe.wait_ge(s.abs_sums, 2)
    pe.matmul(m.ps_k[:, 0:2], m.ones[:, :], m.abs_row[:, :], start=True, stop=True).then_inc(s.abs_total, 1)
    for w, dst in ((0, m.ps_v), (1, m.ps_o)):
        pe.wait_ge(s.ternary, w + 1)
        for c in range(FC):
            last = pe.transpose(dst[:, c * P:(c + 1) * P], m.tern[:, w, c * P:(c + 1) * P], m.ident[:, :])
        last.then_inc(s.ternary_turned, 1)
    pe.wait_ge(s.setup_kept, 3)

    tensor_ffn(pe, m, s, f[0])
    for tick in range(TICKS):
        tensor_tick(pe, m, s, f, 0, tick)
    with pe.Fori(1, LAYERS) as lay:
        for tick in range(TICKS):
            tensor_tick(pe, m, s, f, lay, tick)
    for tick in range(TICKS - 1):
        tensor_tick(pe, m, s, f, LAYERS, tick)
    tensor_ffn(pe, m, s, f[1])


def tensor_tick(pe, m, s, f, lay, tick):
    A, B, C, D = tick_tiles(lay, tick)
    start = lay == 0 if isinstance(lay, int) else False

    def project(T):
        if T.first:
            pe.wait_ge(s.wqkv_loaded, T.layer * (2 * DMA) + 2 * DMA)
        pe.wait_ge(s.x_split, T.n)
        if start and T.first:
            pe.wait_ge(f[0].x_new, NT)
            pe.wait_ge(f[0].ms, NT)
        x_hi, x_lo = m.x_hi[:, T.slot, :], m.x_lo[:, T.slot, :]
        for i, bank, read, done in ((1, m.ps_k, s.elu_k, s.proj_k), (0, m.ps_q, s.elu_q, s.proj_q),
                                    (2, m.ps_v, s.kv_acc, s.proj_v)):
            at_least(pe, read, T.n - 1)
            split_product(pe, bank, m.wqkv[0][:, i, :], m.wqkv[1][:, i, :], x_hi, x_lo).then_inc(done, 1)

    def project_o(T, bank_free):
        if T.first:
            pe.wait_ge(s.wo_loaded, T.layer * DMA + DMA)
        pe.wait_ge(s.v_ready, T.n)
        for sem, n in bank_free:
            at_least(pe, sem, n)
        pe.matmul(m.ps_o[:, :], m.wo[:, :], m.vf[:, T.par, :], start=True, stop=True).then_inc(s.proj_o, 1)

    def up(T, c):
        if c == 0:
            if T.first:
                pe.wait_ge(s.w1_loaded, T.layer * (2 * DMA) + 2 * DMA)
            pe.wait_ge(s.x1_split, T.n)
        at_least(pe, s.gelu_h, T.chunks + (c - 1))
        split_product(pe, m.ps_h[c % 2], m.w1[0][:, c, :], m.w1[1][:, c, :],
                      m.x_hi[:, T.slot, :], m.x_lo[:, T.slot, :]).then_inc(s.ff_up, 1)

    def down(T, c, bank_free):
        if c == 0:
            if T.first:
                pe.wait_ge(s.w2_loaded, T.layer * DMA + DMA)
            for sem, n in bank_free:
                at_least(pe, sem, n)
        pe.wait_ge(s.gelu_h, T.chunks + (c + 1))
        mm = pe.matmul(m.ps_o[:, :], m.w2[:, c, :], m.h[:, T.par, c, :], start=c == 0, stop=c == FC - 1)
        if c == FC - 1:
            mm.then_inc(s.ff_down, 1)

    def turn_y(T, i, free):
        pe.wait_ge((s.y1, s.y2)[i], T.n)
        for sem, n in free:
            at_least(pe, sem, n)
        y = m.y[i][:, T.par, :]
        transpose_tile(pe, m.ps_ty, lambda j: y[:, j * P:(j + 1) * P], m).then_inc((s.turned_y1, s.turned_y2)[i], 1)

    def turn_z(T, i, free):
        pe.wait_ge((s.z1, s.z2)[i], T.n)
        for sem, n in free:
            at_least(pe, sem, n)
        transpose_tile(pe, m.ps_tz, lambda j: m.z[i][:, T.par, j, :], m).then_inc((s.turned_z1, s.turned_z2)[i], 1)

    def b_count(sem, k):
        return [(sem, B[k].n)] if len(B) > k else []

    def c_count(sem, k):
        return [(sem, C[k].n)] if len(C) > k else []

    def d_count(sem, more=0):
        return [(sem, D[0].n + more)] if D else []

    def prior(sem):
        return [(sem, B[0].n - 1 if B else LAYERS * NT)]

    for T in A:
        project(T)
    if B:
        project_o(B[0], d_count(s.gelu_ff))
    if D:
        turn_y(D[0], 1, [(s.z2, D[0].n - 1)] + prior(s.z1))
    if C:
        up(C[0], 0)
        up(C[0], 1)
    if B:
        project_o(B[1], b_count(s.gelu_o, 0))
    if C:
        up(C[0], 2)
        down(C[0], 0, b_count(s.gelu_o, 1) + [(s.gelu_ff, C[0].n - 1)])
    if B:
        turn_y(B[0], 0, d_count(s.z2) + [(s.z1, B[0].n - 1)])
    if C:
        up(C[0], 3)
        down(C[0], 1, [])
    if D:
        turn_z(D[0], 1, [(s.x_full, D[0].n + (NT - 1))] + prior(s.x1_full))
    if C:
        down(C[0], 2, [])
        down(C[0], 3, [])
        up(C[1], 0)
        up(C[1], 1)
    if B:
        turn_y(B[1], 0, b_count(s.z1, 0))
    if C:
        up(C[1], 2)
    if B:
        turn_z(B[0], 0, d_count(s.x_full, NT) + [(s.x1_full, B[0].n - 1)])
    if C:
        down(C[1], 0, c_count(s.gelu_ff, 0))
        up(C[1], 3)
        down(C[1], 1, [])
        turn_y(C[0], 1, b_count(s.z1, 1) + d_count(s.z2))
        down(C[1], 2, [])
    if B:
        turn_z(B[1], 0, b_count(s.x1_full, 0))
    if C:
        down(C[1], 3, [])
        turn_z(C[0], 1, b_count(s.x1_full, 1) + d_count(s.x_full, NT))


def tensor_ffn(pe, m, s, f):
    ps_down = (m.ps_q, m.ps_o)

    def enter(t):
        if f.first:
            return
        pe.wait_ge(s.x_full, LAYERS * NT + t + 1)
        at_least(pe, f.x_in, t)
        transpose_tile(pe, m.ps_k, lambda j: m.x_fm[:, t, j * P:(j + 1) * P], m).then_inc(f.turned_x, 1)

    def turn(t):
        pe.wait_ge(f.z, t + 1)
        at_least(pe, f.z_lo, t)
        if t == 0 and not f.first:
            pe.wait_ge(s.z2, LAYERS * NT)
            pe.wait_ge(s.gelu_h, LAYERS * NT * FC)
        transpose_tile(pe, m.ps_ty, lambda j: m.fz[:, t % 2, j, :], m).then_inc(f.turned_z, 1)

    def up(t):
        pe.wait_ge(f.z_lo, t + 1)
        for c in range(FC):
            at_least(pe, f.gelu, FC * t + c - 1)
            pe.matmul(m.ps_h[c % 2][:, :], m.upT[:, c, :], m.zc[0][:, t % 2, :], start=True, stop=False)
            pe.matmul(m.ps_h[c % 2][:, :], m.upT[:, c, :], m.zc[1][:, t % 2, :], start=False,
                      stop=True).then_inc(f.up, 1)

    def down(t):
        at_least(pe, f.x_new, t - 1)
        if t == 0 and not f.first:
            pe.wait_ge(s.gelu_ff, LAYERS * NT)
            pe.wait_ge(s.elu_q, LAYERS * NT)
        pe.wait_ge(f.gelu, FC * (t + 1))
        for j in range(BLK):
            for c in range(FC):
                last = pe.matmul(ps_down[t % 2][:, j * P:(j + 1) * P], m.h[:, t % 2, c, j * P:(j + 1) * P],
                                 m.downT[:, c, :], start=c == 0, stop=c == FC - 1)
        last.then_inc(f.down, 1)

    def squares(t):
        pe.wait_ge(f.hss, t + 1)
        at_least(pe, f.ms, t)
        for j in range(BLK):
            last = pe.matmul(m.ps_v[:, j:j + 1], m.hss[:, t % 2, j * P:(j + 1) * P], m.ones[:, 0:1],
                             start=True, stop=True)
        last.then_inc(f.ssq, 1)

    def turn_c(t):
        pe.wait_ge(f.z_c, t + 1)
        at_least(pe, s.x_full, t)
        transpose_tile(pe, m.ps_tz, lambda j: m.z[0][:, t % 2, j, :], m).then_inc(f.turned_c, 1)

    for t in range(NT + 2):
        if t < NT:
            enter(t)
            turn(t)
        if 1 <= t <= NT:
            up(t - 1)
            down(t - 1)
            squares(t - 1)
        if t >= 2 and f.first:
            turn_c(t - 2)



def scalar_engine(act, m, s, f):
    scalar_ffn(act, m, s, f[0])
    for tick in range(TICKS):
        scalar_tick(act, m, s, 0, tick)
    with act.Fori(1, LAYERS) as lay:
        for tick in range(TICKS):
            scalar_tick(act, m, s, lay, tick)
    for tick in range(TICKS - 1):
        scalar_tick(act, m, s, LAYERS, tick)
    scalar_ffn(act, m, s, f[1])


def scalar_tick(act, m, s, lay, tick):
    A, B, C, D = tick_tiles(lay, tick)

    def log_den(T):
        wait_apart(act, s, s.den_ready, T.n)
        act.activation(m.rec[:, T.par, :], m.den[:, T.par, :], ACT.Ln, bias=m.eps[:, 0:1]).then_inc(s.log_den, 1)

    def recip(T):
        wait_apart(act, s, s.log_den, T.n)
        act.activation(m.rec[:, T.par, :], m.rec[:, T.par, :], ACT.Exp, scale=-1.0).then_inc(s.recip, 1)

    def exp(T, which):
        e, neg, done = ((m.e_k, s.neg_k, s.exp_k), (m.e_q, s.neg_q, s.exp_q))[which]
        wait_apart(act, s, neg, T.n)
        act.activation(e[:, T.par, :], e[:, T.par, :], ACT.Exp).then_inc(done, 1)

    def sum_k(T):
        wait_apart(act, s, s.elu_k, T.n)
        for b in range(2):
            cols = slice(b * SEQ, (b + 1) * SEQ)
            act.activation(m.kf[:, T.par, cols], m.elu_k[:, T.par, cols], ACT.Identity, bias=1.0,
                           accum_out=m.ksum[:, T.par, b:b + 1]).then_inc(s.ksum, 1)

    def gelu(T, bank, ready, n, dst, bias, done):
        wait_apart(act, s, ready, n)
        act.activation(dst, bank[:, :], ACT.Gelu_apprx_tanh, bias=bias).then_inc(done, 1)

    def gelu_o(T):
        gelu(T, m.ps_o, s.proj_o, T.n, m.y[0][:, T.par, :], column(m, BO, T.layer), s.gelu_o)

    def gelu_h(T, c):
        gelu(T, m.ps_h[c % 2], s.ff_up, T.chunks + (c + 1), m.h[:, T.par, c, :],
             column(m, B1, T.layer, c, FC), s.gelu_h)

    def gelu_ff(T):
        gelu(T, m.ps_o, s.ff_down, T.n, m.y[1][:, T.par, :], column(m, B2, T.layer), s.gelu_ff)

    def full(T, i):
        wait_apart(act, s, (s.turned_z1, s.turned_z2)[i], T.n)
        act.activation(m.x_fm[:, T.slot, :], m.ps_tz[:, :], ACT.Identity,
                       bias=column(m, (LN1B, LN2B)[i], T.layer),
                       scale=column(m, (LN1S, LN2S)[i], T.layer)).then_inc((s.x1_full, s.x_full)[i], 1)

    if B:
        log_den(B[0])
    if A:
        exp(A[0], 0)
    if B:
        log_den(B[1])
    if A:
        exp(A[0], 1)
    for T in B:
        recip(T)
    if A:
        exp(A[1], 0)
        sum_k(A[0])
        exp(A[1], 1)
        sum_k(A[1])
    if B:
        gelu_o(B[0])
    if C:
        gelu_h(C[0], 0)
        gelu_h(C[0], 1)
    if B:
        gelu_o(B[1])
    if C:
        gelu_h(C[0], 2)
        gelu_h(C[0], 3)
    if D:
        full(D[0], 1)
    if C:
        gelu_ff(C[0])
        gelu_h(C[1], 0)
        gelu_h(C[1], 1)
        gelu_h(C[1], 2)
    if B:
        full(B[0], 0)
    if C:
        gelu_h(C[1], 3)
    if B:
        full(B[1], 0)
    if C:
        gelu_ff(C[1])
        full(C[0], 1)


def scalar_ffn(act, m, s, f):
    def z_hi(t):
        act.wait_ge(f.turned_z, t + 1)
        act.activation(m.zc[0][:, t % 2, :], m.ps_ty[:, :], ACT.Copy).then_inc(f.z_hi, 1)

    def gelu(t):
        for c in range(FC):
            act.wait_ge(f.up, FC * t + c + 1)
            if t >= 2 and c == 0:
                act.wait_ge(f.down, t - 1)
                act.wait_ge(f.hsq, t - 1)
            act.activation(m.h[:, t % 2, c, :], m.ps_h[c % 2][:, :], ACT.Gelu).then_inc(f.gelu, 1)

    def full(t):
        act.wait_ge(f.turned_c, t + 1)
        act.activation(m.x_fm[:, t, :], m.ps_tz[:, :], ACT.Copy).then_inc(s.x_full, 1)

    for t in range(NT + 2):
        if t < NT:
            z_hi(t)
        if 1 <= t <= NT:
            gelu(t - 1)
        if t >= 2 and f.first:
            full(t - 2)



def block_stats(dve, src, st, done):
    for j in range(BLK):
        last = dve.bn_stats(st[:, j, :], src(j))
    last.then_inc(done, 1)


def block_means(dve, s, st, mv, ready, n, done):
    wait_apart(dve, s, ready, n)
    for j in range(BLK):
        last = dve.bn_aggr(mv[:, j, :], st[:, j, :])
    last.then_inc(done, 1)


def normalise(dve, dst, src, mv, scale, done):
    for j in range(BLK):
        last = dve.tensor_scalar(dst[:, j, :], src(j), mv[:, j, 0:1], scale[:, j:j + 1], ALU.subtract, ALU.mult)
    last.then_inc(done, 1)


def vector_engine(dve, m, s, f):
    dve.wait_ge(s.setup_loaded, DMA * 13)
    for w in range(2):
        dve.tensor_reduce(m.abs_row[:, w:w + 1], m.raw_tern[:, w, :], AX_X, ALU.add,
                          apply_absolute_value=True).then_inc(s.abs_sums, 1)
    dve.wait_ge(s.abs_total, 1)
    for i, half in enumerate((0.5, -0.5)):
        dve.tensor_scalar(m.thr[:, i, :], m.ps_k[:, 0:2], 1.0 / (FF * P), half, ALU.mult,
                          ALU.mult).then_inc(s.thresholds, 1)
    dve.wait_ge(s.thresholds, 2)
    for w in range(2):
        dve.tensor_scalar(m.below[:, w, :], m.raw_tern[:, w, :], m.thr[:, 1, w:w + 1], None,
                          ALU.is_lt).then_inc(s.above, 1)
    for w in range(2):
        dve.wait_ge(s.above, w + 1)
        dve.scalar_tensor_tensor(m.tern[:, w, :], m.raw_tern[:, w, :], m.thr[:, 0, w:w + 1], m.below[:, w, :],
                                 ALU.is_gt, ALU.subtract).then_inc(s.ternary, 1)
    dve.wait_ge(s.par_turned, 1)
    dve.tensor_copy(m.par[:, :], m.ps_q[:, 0:NPAR]).then_inc(s.setup_kept, 1)
    for w, dst, bank in ((0, m.upT, m.ps_v), (1, m.downT, m.ps_o)):
        dve.wait_ge(s.ternary_turned, w + 1)
        dve.tensor_copy(dst[:, :, :].rearrange("p c d -> p (c d)"), bank[:, :]).then_inc(s.setup_kept, 1)

    vector_ffn(dve, m, s, f[0])
    for tick in range(TICKS):
        vector_tick(dve, m, s, 0, tick)
    with dve.Fori(1, LAYERS) as lay:
        for tick in range(TICKS):
            vector_tick(dve, m, s, lay, tick)
    for tick in range(TICKS - 1):
        vector_tick(dve, m, s, LAYERS, tick)
    vector_ffn(dve, m, s, f[1])


def vector_tick(dve, m, s, lay, tick):
    A, B, C, D = tick_tiles(lay, tick)

    def negative(T, which):
        e, bank, base, proj, done = ((m.e_k, m.ps_k, BK, s.proj_k, s.neg_k), (m.e_q, m.ps_q, BQ, s.proj_q, s.neg_q))[which]
        dve.wait_ge(proj, T.n)
        dve.tensor_scalar(e[:, T.par, :], bank[:, :], column(m, base, T.layer), 0.0, ALU.add, ALU.min).then_inc(done, 1)

    def elu(T, which):
        e, bank, dst, base, exp, expm1, done = (
            (m.e_k, m.ps_k, m.elu_k, BK, s.exp_k, s.expm1_k, s.elu_k),
            (m.e_q, m.ps_q, m.elu_q, BQ, s.exp_q, s.expm1_q, s.elu_q))[which]
        dve.wait_ge(exp, T.n)
        dve.tensor_scalar(e[:, T.par, :], e[:, T.par, :], 1.0, None, ALU.subtract).then_inc(expm1, 1)
        at_least(dve, s.num_ready, T.n - 2)
        dve.wait_ge(expm1, T.n)
        dve.scalar_tensor_tensor(dst[:, T.par, :], bank[:, :], column(m, base, T.layer), e[:, T.par, :],
                                 ALU.add, ALU.max).then_inc(done, 1)

    def sum_kv(T):
        dve.wait_ge(s.elu_k, T.n)
        dve.wait_ge(s.proj_v, T.n)
        for b in range(2):
            cols = slice(b * SEQ, (b + 1) * SEQ)
            last = dve.scalar_tensor_tensor(m.kvf[:, T.par, cols], m.elu_k[:, T.par, cols], 1.0, m.ps_v[:, cols],
                                            ALU.add, ALU.mult, accum_out=m.kvacc[:, T.par, b:b + 1])
        last.then_inc(s.kv_acc, 1)

    def kv(T):
        dve.wait_ge(s.ksum, T.n * 2)
        dve.wait_ge(s.kv_acc, T.n)
        dve.scalar_tensor_tensor(m.kv[:, T.par, :], m.ksum[:, T.par, :], column(m, BV, T.layer),
                                 m.kvacc[:, T.par, :], ALU.mult, ALU.add).then_inc(s.kv_ready, 1)

    def newton_a(T):
        dve.wait_ge(s.recip, T.n)
        dve.scalar_tensor_tensor(m.nwt[:, T.par, :], m.den[:, T.par, :], EPS_ATTN, m.rec[:, T.par, :],
                                 ALU.add, ALU.mult).then_inc(s.newton_a, 1)

    def newton_c(T):
        dve.wait_ge(s.newton_a, T.n)
        dve.scalar_tensor_tensor(m.rec[:, T.par, :], m.nwt[:, T.par, :], 2.0, m.rec[:, T.par, :],
                                 ALU.subtract, ALU.mult).then_inc(s.newton_c, 1)

    def newton_v(T):
        dve.wait_ge(s.num_ready, T.n)
        dve.wait_ge(s.newton_c, T.n)
        dve.scalar_tensor_tensor(m.vf[:, T.par, :], m.num[:, T.par, :], -1.0, m.rec[:, T.par, :],
                                 ALU.mult, ALU.mult).then_inc(s.v_ready, 1)

    def source(j):
        return m.ps_ty[:, j * P:(j + 1) * P]

    def stats(T, i):
        dve.wait_ge((s.turned_y1, s.turned_y2)[i], T.n)
        block_stats(dve, source, m.st[i][:, T.par], (s.stats1, s.stats2)[i])
        block_means(dve, s, m.st[i][:, T.par], m.mv[i][:, T.par], (s.stats1, s.stats2)[i], T.n, (s.mv1, s.mv2)[i])

    def z(T, i):
        dve.wait_ge((s.rstd1, s.rstd2)[i], T.n)
        normalise(dve, m.z[i][:, T.par], source, m.mv[i][:, T.par], m.rstd[i][:, T.par], (s.z1, s.z2)[i])

    def hi(T, i):
        full, done, more = ((s.x1_full, s.x1_hi, 0), (s.x_full, s.x_hi, NT))[i]
        dve.wait_ge(full, T.n + more)
        dve.tensor_copy(m.x_hi[:, T.slot, :], m.x_fm[:, T.slot, :]).then_inc(done, 1)

    for k in range(2):
        if A:
            negative(A[k], 0)
            negative(A[k], 1)
            elu(A[k], 0)
            elu(A[k], 1)
            sum_kv(A[k])
        if B:
            newton_a(B[k])
            newton_c(B[k])
            newton_v(B[k])
    for T in A:
        kv(T)
    if D:
        stats(D[0], 1)
        z(D[0], 1)
    if B:
        stats(B[0], 0)
    if B:
        z(B[0], 0)
    if D:
        hi(D[0], 1)
    if B:
        stats(B[1], 0)
        z(B[1], 0)
        hi(B[0], 0)
    if C:
        stats(C[0], 1)
        z(C[0], 1)
    if B:
        hi(B[1], 0)
    if C:
        hi(C[0], 1)


def vector_ffn(dve, m, s, f):
    eps_var, rstd, sd, den, recip, alpha, ms, beta = range(8)

    def source(t):
        return lambda j: m.x_tm[:, t, j, :]

    def enter(t):
        if f.first:
            dve.wait_ge(f.loaded, DMA * (t + 1))
        else:
            dve.wait_ge(f.turned_x, t + 1)
            x = m.x_tm[:, t, :, :].rearrange("p j d -> p (j d)")
            dve.tensor_tensor(x, m.ps_k[:, :], x, ALU.add).then_inc(f.x_in, 1)
            dve.wait_ge(f.x_in, t + 1)
        block_stats(dve, source(t), m.fst[:, t % 2], f.stats)
        block_means(dve, s, m.fst[:, t % 2], m.fmv[:, t % 2], f.stats, t + 1, f.mv)

    def normal(t):
        sc = m.scale[:, t % 2]
        dve.wait_ge(f.den, t + 1)
        dve.reciprocal(sc[:, recip, :], sc[:, den, :]).then_inc(f.recip, 1)
        dve.wait_ge(f.recip, t + 1)
        dve.tensor_tensor(sc[:, alpha, :], sc[:, recip, :], sc[:, rstd, :], ALU.mult).then_inc(f.alpha, 1)
        dve.wait_ge(f.alpha, t + 1)
        normalise(dve, m.fz[:, t % 2], source(t), m.fmv[:, t % 2], sc[:, alpha, :], f.z)

    def low(t):
        dve.wait_ge(f.z_hi, t + 1)
        dve.tensor_tensor(m.zc[1][:, t % 2, :], m.ps_ty[:, :], m.zc[0][:, t % 2, :].bitcast(F32),
                          ALU.subtract).then_inc(f.z_lo, 1)

    def sum_squares(t):
        dve.wait_ge(f.hsq, t + 1)
        at_least(dve, f.ssq, t - 1)
        dve.tensor_reduce(m.hss[:, t % 2, :], m.hsq[:, t % 2, :, :].rearrange("p c t -> p t c"), AX_X,
                          ALU.add).then_inc(f.hss, 1)
        dve.wait_ge(f.ssq, t + 1)
        dve.tensor_scalar(m.scale[:, t % 2, ms, :], m.ps_v[:, 0:BLK], 1.0 / FF, None, ALU.mult).then_inc(f.ms, 1)

    def residual(t):
        sc = m.scale[:, t % 2]
        dve.wait_ge(f.rms_eps, t + 1)
        dve.reciprocal(sc[:, ms, :], sc[:, ms, :]).then_inc(f.rms_recip, 1)
        dve.wait_ge(f.rms_recip, t + 1)
        dve.tensor_scalar(sc[:, beta, :], sc[:, ms, :], 0.5, None, ALU.mult).then_inc(f.beta, 1)
        dve.wait_ge(f.beta, t + 1)
        dve.wait_ge(f.down, t + 1)
        bank = (m.ps_q, m.ps_o)[t % 2]
        for j in range(BLK):
            last = dve.scalar_tensor_tensor(m.x_tm[:, t, j, :], bank[:, j * P:(j + 1) * P], sc[:, beta, j:j + 1],
                                            m.x_tm[:, t, j, :], ALU.mult, ALU.add)
        last.then_inc(f.x_new, 1)

    def to_attention(t):
        dve.wait_ge(f.x_new, t + 1)
        block_stats(dve, source(t), m.st[0][:, t % 2], f.stats_c)
        block_means(dve, s, m.st[0][:, t % 2], m.mv[0][:, t % 2], f.stats_c, t + 1, f.mv_c)
        dve.wait_ge(f.rstd_c, t + 1)
        normalise(dve, m.z[0][:, t % 2], source(t), m.mv[0][:, t % 2], m.rstd[0][:, t % 2], f.z_c)

    def hi(t):
        dve.wait_ge(s.x_full, t + 1)
        dve.tensor_copy(m.x_hi[:, t, :], m.x_fm[:, t, :]).then_inc(s.x_hi, 1)

    for t in range(NT + 2):
        if t < NT:
            enter(t)
            normal(t)
            low(t)
        if 1 <= t <= NT:
            sum_squares(t - 1)
            residual(t - 1)
        if f.first and 1 <= t <= NT:
            to_attention(t - 1)
        if f.first and t >= 2:
            hi(t - 2)



def gpsimd_engine(pool, m, s, f):
    pool.memset(m.ones[:, :], 1.0)
    pool.memset(m.eps[:, :], EPS_ATTN)
    pool.memset(m.minus_half[:, :], -0.5)
    pool.memset(m.plus_half[:, :], 0.5).then_inc(s.consts, 1)
    pool.wait_ge(s.consts, 1)
    split_weights(pool, m, s, 0)
    gpsimd_ffn(pool, m, s, f[0])
    for tick in range(TICKS - 1):
        gpsimd_tick(pool, m, s, 0, tick)
    with pool.Fori(1, LAYERS) as lay:
        gpsimd_tick(pool, m, s, lay, -1)
        split_weights(pool, m, s, lay)
        for tick in range(TICKS - 1):
            gpsimd_tick(pool, m, s, lay, tick)
    for tick in range(-1, TICKS - 1):
        gpsimd_tick(pool, m, s, LAYERS, tick)
    gpsimd_ffn(pool, m, s, f[1])


def split_weights(pool, m, s, lay):
    for raw, pair, loaded, per, hi, done, moved in (
            (m.raw_qkv, m.next_qkv, s.raw_qkv_loaded, 3, s.raw_qkv_hi, s.next_qkv_split, s.wqkv_loaded),
            (m.raw_w1, m.next_w1, s.raw_w1_loaded, 1, s.raw_w1_hi, s.next_w1_split, s.w1_loaded)):
        wait_apart(pool, s, loaded, lay * (per * DMA) + per * DMA)
        if not isinstance(lay, int):
            wait_apart(pool, s, moved, lay * (2 * DMA))
        pool.tensor_copy(pair[0][:, :, :], raw[:, :, :]).then_inc(hi, 1)
        wait_apart(pool, s, hi, lay + 1)
        pool.tensor_tensor(pair[1][:, :, :], raw[:, :, :], pair[0][:, :, :].bitcast(F32),
                           ALU.subtract).then_inc(done, 1)


def inverse_root(pool, m, s, dst, tmp, var, eps, ready, n, mid, done):
    wait_apart(pool, s, ready, n)
    pool.tensor_scalar(tmp, var, eps, None, ALU.add).then_inc(mid, 1)
    wait_apart(pool, s, mid, n)
    pool.tensor_tensor(dst, tmp, m.minus_half[:, :], ALU.pow).then_inc(done, 1)


def gpsimd_tick(pool, m, s, lay, tick):
    A, B, C, D = tick_tiles(lay, tick)

    def add_residual(T, i):
        wait_apart(pool, s, (s.gelu_o, s.gelu_ff)[i], T.n)
        y = m.y[i][:, T.par, :]
        pool.tensor_tensor(y, y, m.x_fm[:, T.slot, :], ALU.add).then_inc((s.y1, s.y2)[i], 1)

    def rstd(T, i):
        inverse_root(pool, m, s, m.rstd[i][:, T.par, :], m.ve[i][:, T.par, :], m.mv[i][:, T.par, :, 1], EPS_LN,
                     (s.mv1, s.mv2)[i], T.n, (s.ve1, s.ve2)[i], (s.rstd1, s.rstd2)[i])

    def low(T, i):
        hi, done, more = ((s.x1_hi, s.x1_split, 0), (s.x_hi, s.x_split, NT))[i]
        wait_apart(pool, s, hi, T.n + more)
        pool.tensor_tensor(m.x_lo[:, T.slot, :], m.x_fm[:, T.slot, :], m.x_hi[:, T.slot, :].bitcast(F32),
                           ALU.subtract).then_inc(done, 1)

    def ratio(T):
        for sums, dst, elu_q, ready, n, done in ((m.ksum, m.den, s.elu_q, s.ksum, T.n * 2, s.den_ready),
                                                 (m.kv, m.num, s.elu_q, s.kv_ready, T.n, s.num_ready)):
            wait_apart(pool, s, elu_q, T.n)
            wait_apart(pool, s, ready, n)
            for b in range(2):
                cols = slice(b * SEQ, (b + 1) * SEQ)
                last = pool.tensor_scalar(dst[:, T.par, cols], m.elu_q[:, T.par, cols], 1.0, sums[:, T.par, b:b + 1],
                                          ALU.add, ALU.mult)
            last.then_inc(done, 1)

    for T in D:
        add_residual(T, 1)
    if B:
        add_residual(B[0], 0)
    for T in D:
        rstd(T, 1)
    if B:
        rstd(B[0], 0)
        add_residual(B[1], 0)
    for T in D:
        low(T, 1)
    if B:
        rstd(B[1], 0)
    if C:
        add_residual(C[0], 1)
    if B:
        low(B[0], 0)
    if C:
        rstd(C[0], 1)
    if B:
        low(B[1], 0)
    for T in A:
        ratio(T)
    if C:
        low(C[0], 1)


def gpsimd_ffn(pool, m, s, f):
    eps_var, rstd, sd, den, recip, alpha, ms, beta = range(8)

    def scales(t):
        sc = m.scale[:, t % 2]
        var = m.fmv[:, t % 2, :, 1]
        inverse_root(pool, m, s, sc[:, rstd, :], sc[:, eps_var, :], var, EPS_OUTER, f.mv, t + 1, f.var_eps, f.rstd)
        pool.tensor_tensor(sc[:, sd, :], var, m.plus_half[:, :], ALU.pow).then_inc(f.sd, 1)
        pool.wait_ge(f.sd, t + 1)
        pool.wait_ge(f.rstd, t + 1)
        pool.tensor_tensor(sc[:, sd, :], sc[:, sd, :], sc[:, rstd, :], ALU.mult).then_inc(f.sd_rstd, 1)
        pool.wait_ge(f.sd_rstd, t + 1)
        pool.tensor_scalar(sc[:, den, :], sc[:, sd, :], EPS_RMS, None, ALU.add).then_inc(f.den, 1)

    def squares(t):
        pool.wait_ge(f.gelu, FC * (t + 1))
        at_least(pool, f.hss, t - 1)
        pool.tensor_tensor(m.hsq[:, t % 2, :, :], m.h[:, t % 2, :, :], m.h[:, t % 2, :, :], ALU.mult).then_inc(f.hsq, 1)

    def rms(t):
        sc = m.scale[:, t % 2]
        pool.wait_ge(f.ms, t + 1)
        pool.tensor_tensor(sc[:, ms, :], sc[:, ms, :], m.plus_half[:, :], ALU.pow).then_inc(f.rms, 1)
        pool.wait_ge(f.rms, t + 1)
        pool.tensor_scalar(sc[:, ms, :], sc[:, ms, :], EPS_RMS, None, ALU.add).then_inc(f.rms_eps, 1)

    def rstd_c(t):
        inverse_root(pool, m, s, m.rstd[0][:, t % 2, :], m.ve[0][:, t % 2, :], m.mv[0][:, t % 2, :, 1], EPS_OUTER,
                     f.mv_c, t + 1, f.ve_c, f.rstd_c)

    def low(t):
        pool.wait_ge(s.x_hi, t + 1)
        pool.tensor_tensor(m.x_lo[:, t, :], m.x_fm[:, t, :], m.x_hi[:, t, :].bitcast(F32),
                           ALU.subtract).then_inc(s.x_split, 1)

    for t in range(NT + 2):
        if t < NT:
            scales(t)
        if 1 <= t <= NT:
            squares(t - 1)
            rms(t - 1)
        if f.first and 1 <= t <= NT:
            rstd_c(t - 1)
        if f.first and t >= 2:
            low(t - 2)


_INS = ["x", "Wq", "bq", "Wk", "bk", "Wv", "bv", "Wo", "bo", "ln1_s", "ln1_b", "W1", "b1", "W2", "b2",
        "ln2_s", "ln2_b"]
_FFN = ["w_up", "w_down"]


def kernel(**inputs):
    import numpy as np
    import concourse.bacc as bacc
    from concourse.bass_utils import run_bass_kernel_spmd

    nc = bacc.Bacc("TRN2", target_bir_lowering=False, num_devices=1)
    given = [(n, inputs[f"L0_attn_{n}"]) for n in _INS] + [(n, inputs[f"L0_ffn_{n}"]) for n in _FFN]
    given.append(("identity", np.eye(P, dtype=np.float32)))
    arrays, args = {}, []
    for name, value in given:
        a = np.ascontiguousarray(value)
        arrays[f"in_{name}"] = a
        args.append(nc.dram_tensor(f"in_{name}", a.shape, mybir.dt.from_np(a.dtype), kind="ExternalInput").ap())
    x = arrays["in_x"]
    args.append(nc.dram_tensor("out_0", x.shape, F32, kind="ExternalOutput").ap())
    macaron(nc, *args)
    return run_bass_kernel_spmd(nc, [arrays], core_ids=[0]).results[0]["out_0"]
```

```python
from contextlib import ExitStack

import concourse.bass as bass
from concourse import mybir

P = 128
LAYERS = 8
SEQ = 256
TILE = 2 * SEQ
NT = 8
BLK = TILE // P
FC = 4
FF = FC * P
PAIRS = LAYERS // 2
TICKS = NT // 2
LAG = 4
KEY, QUERY, VALUE = 0, 1, 2
EXP_AND_LN = "natural_log_exp_and_others"

EPS_ATTN = 1e-6
EPS_LN = 1e-6
EPS_OUTER = 1e-5
EPS_RMS = 1e-8

F32 = mybir.dt.float32
F32R = mybir.dt.float32r
ALU = mybir.AluOpType
ACT = mybir.ActivationFunctionType
AX_X = mybir.AxisListType.X

BQ, BK, BV, BO, LN1S, LN1B, B2, LN2S, LN2B, B1 = (LAYERS * k for k in range(10))
NPAR = B1 + FC * LAYERS
NEG_BQ, NEG_BK = NPAR, NPAR + LAYERS
DMA = 16


class Shared:
    pass


class Tile:

    def __init__(self, pair, rel):
        self.n = pair * (2 * NT) + (rel + 1)
        self.layer = pair * 2 + rel // NT
        self.weights = (rel // NT) % 2
        self.loads = pair + (rel // (2 * NT) + 1)
        self.slot = rel % NT
        self.par = rel % 2
        self.chunks = pair * (2 * NT * FC) + rel * FC
        self.first = rel % NT == 0


def tiles_of(pair, tick):
    def t(k, lag):
        rel = 2 * (tick - lag) + k
        if isinstance(pair, int) and not 0 <= pair * (2 * NT) + rel < LAYERS * NT:
            return None
        return Tile(pair, rel)

    def n(k, lag):
        count = pair * (2 * NT) + (2 * (tick - lag) + k + 1)
        return max(0, min(LAYERS * NT, count)) if isinstance(pair, int) else count
    return t, n


def at_least(eng, sem, value):
    if not isinstance(value, int) or value > 0:
        eng.wait_ge(sem, value)


def bank_left(eng, sem, value, other=None, other_value=0):
    if other is None or isinstance(other_value, int):
        at_least(eng, sem, value)
    if other is not None:
        at_least(eng, other, other_value)


def wait_apart(eng, s, sem, value):
    if not isinstance(value, int):
        value = eng.to_reg(value)
        eng.wait_ge(s.consts, 1)
    eng.wait_ge(sem, value)


def column(m, base, layer, k=0, per=1):
    if isinstance(layer, int):
        c = base + layer * per + k
        return m.par[:, c:c + 1]
    return m.par[:, bass.ds(layer * per + (base + k), 1)]


def macaron(nc, x_in, Wq, bq, Wk, bk, Wv, bv, Wo, bo, ln1_s, ln1_b, W1, b1, W2, b2, ln2_s, ln2_b,
            w_up, w_down, ident_in, out):
    x_rows = x_in.rearrange("b s d -> (b s) d").rearrange("(t j p) d -> t p j d", j=BLK, p=P)
    out_rows = out.rearrange("b s d -> (b s) d").rearrange("(t j p) d -> t p j d", j=BLK, p=P)
    W2_rows = W2.rearrange("l (c p) d -> l p c d", p=P)

    with ExitStack() as ctx:
        m, s = Shared(), Shared()

        def sb(name, shape, dt=F32):
            return ctx.enter_context(nc.sbuf_tensor(name, [P] + shape, dt))

        def sem(name):
            return ctx.enter_context(nc.semaphore(name))

        bank = [ctx.enter_context(nc.psum_tensor(f"bank{i}", [P, TILE], F32)) for i in range(8)]
        m.ps_q, m.ps_k, m.ps_v, m.ps_o, m.ps_h0, m.ps_h1, m.ps_ty, m.ps_tz = bank
        m.ps_h = (m.ps_h0, m.ps_h1)

        m.ident = sb("ident", [P])
        m.ones = sb("ones", [P])
        m.eps = sb("eps", [1])
        m.minus_half = sb("minus_half", [BLK])
        m.plus_half = sb("plus_half", [BLK])
        m.x_tm = sb("x_tm", [NT, BLK, P])
        m.x_fm = sb("x_fm", [NT, TILE])
        m.x_hi = sb("x_hi", [NT, TILE], F32R)
        m.x_lo = sb("x_lo", [NT, TILE], F32R)
        m.par_rows = sb("par_rows", [P])
        m.par = sb("par", [NPAR + 2 * LAYERS])
        m.upT = sb("upT", [FC, P], F32R)
        m.downT = sb("downT", [FC, P])
        m.wqkv = [[sb(f"wqkv{i}_{x}", [3, P], F32R) for x in ("hi", "lo")] for i in range(2)]
        m.w1 = [[sb(f"w1{i}_{x}", [FC, P], F32R) for x in ("hi", "lo")] for i in range(2)]
        m.wo = [sb(f"wo{i}", [P]) for i in range(2)]
        m.w2 = [sb(f"w2{i}", [FC, P]) for i in range(2)]
        m.raw_qkv = sb("raw_qkv", [3, P])
        m.raw_w1 = sb("raw_w1", [FC, P])

        m.e_k = sb("e_k", [2, TILE])
        m.e_q = sb("e_q", [2, TILE])
        m.elu_k = sb("elu_k", [2, TILE])
        m.elu_q = sb("elu_q", [2, TILE])
        m.kf = sb("kf", [2, TILE])
        m.kvf = sb("kvf", [2, TILE])
        m.ksum = sb("ksum", [2, 2])
        m.kvacc = sb("kvacc", [2, 2])
        m.kv = sb("kv", [2, 2])
        m.den = sb("den", [2, TILE])
        m.num = sb("num", [2, TILE])
        m.rec = sb("rec", [2, TILE])
        m.nwt = sb("nwt", [2, TILE])
        m.vf = sb("vf", [2, TILE])
        m.y = [sb(f"y{i}", [2, TILE]) for i in (1, 2)]
        m.z = [sb(f"z{i}", [2, BLK, P]) for i in (1, 2)]
        m.st = [sb(f"st{i}", [2, BLK, 6]) for i in (1, 2)]
        m.mv = [sb(f"mv{i}", [2, BLK, 2]) for i in (1, 2)]
        m.ve = [sb(f"ve{i}", [2, BLK]) for i in (1, 2)]
        m.rstd = [sb(f"rstd{i}", [2, BLK]) for i in (1, 2)]
        m.h = sb("h", [2, FC, TILE])

        s.setup_loaded = sem("setup_loaded")
        s.consts = sem("consts")
        s.abs_sums = sem("abs_sums")
        s.abs_total = sem("abs_total")
        s.thresholds = sem("thresholds")
        s.above = sem("above")
        s.ternary = sem("ternary")
        s.ternary_turned = sem("ternary_turned")
        s.par_turned = sem("par_turned")
        s.setup_kept = sem("setup_kept")
        s.raw_qkv_loaded = sem("raw_qkv_loaded")
        s.raw_w1_loaded = sem("raw_w1_loaded")
        s.wo_loaded = [sem(f"wo{i}_loaded") for i in range(2)]
        s.w2_loaded = [sem(f"w2{i}_loaded") for i in range(2)]
        s.raw_qkv_hi = sem("raw_qkv_hi")
        s.raw_w1_hi = sem("raw_w1_hi")
        s.qkv_split = sem("qkv_split")
        s.w1_split = sem("w1_split")
        s.proj_k = sem("proj_k")
        s.proj_q = sem("proj_q")
        s.proj_v = sem("proj_v")
        s.proj_o = sem("proj_o")
        s.ff_up = sem("ff_up")
        s.ff_down = sem("ff_down")
        s.turned_y1 = sem("turned_y1")
        s.turned_z1 = sem("turned_z1")
        s.turned_y2 = sem("turned_y2")
        s.turned_z2 = sem("turned_z2")
        s.exp_k = sem("exp_k")
        s.exp_q = sem("exp_q")
        s.ksum = sem("ksum")
        s.log_den = sem("log_den")
        s.recip = sem("recip")
        s.gelu_o = sem("gelu_o")
        s.gelu_h = sem("gelu_h")
        s.gelu_ff = sem("gelu_ff")
        s.x1_full = sem("x1_full")
        s.x_full = sem("x_full")
        s.neg_k = sem("neg_k")
        s.neg_q = sem("neg_q")
        s.expm1_k = sem("expm1_k")
        s.expm1_q = sem("expm1_q")
        s.elu_k = sem("elu_k")
        s.elu_q = sem("elu_q")
        s.kv_acc = sem("kv_acc")
        s.kv_ready = sem("kv_ready")
        s.newton_a = sem("newton_a")
        s.newton_c = sem("newton_c")
        s.v_ready = sem("v_ready")
        s.stats1 = sem("stats1")
        s.mv1 = sem("mv1")
        s.z1 = sem("z1")
        s.x1_hi = sem("x1_hi")
        s.stats2 = sem("stats2")
        s.mv2 = sem("mv2")
        s.z2 = sem("z2")
        s.x_hi = sem("x_hi")
        s.den_ready = sem("den_ready")
        s.num_ready = sem("num_ready")
        s.y1 = sem("y1")
        s.y2 = sem("y2")
        s.ve1 = sem("ve1")
        s.ve2 = sem("ve2")
        s.rstd1 = sem("rstd1")
        s.rstd2 = sem("rstd2")
        s.x1_split = sem("x1_split")
        s.x_split = sem("x_split")

        f = [ffn_buffers(sb, sem, m, tag) for tag in ("in", "out")]
        d = Shared()
        d.x_rows, d.out_rows, d.ident, d.w_up, d.w_down = x_rows, out_rows, ident_in, w_up, w_down
        d.kqv, d.Wo, d.W1, d.W2, d.b1 = (Wk, Wq, Wv), Wo, W1, W2_rows, b1
        d.vectors = ((BQ, bq), (BK, bk), (BV, bv), (BO, bo), (LN1S, ln1_s), (LN1B, ln1_b), (B2, b2),
                     (LN2S, ln2_s), (LN2B, ln2_b))

        block = ctx.enter_context(nc.Block())

        @block.sync
        def _(sp):
            sync_engine(sp, m, s, f, d)

        @block.tensor
        def _(pe):
            tensor_engine(pe, m, s, f)

        @block.scalar
        def _(act):
            scalar_engine(act, m, s, f)

        @block.vector
        def _(dve):
            vector_engine(dve, m, s, f)

        @block.gpsimd
        def _(pool):
            gpsimd_engine(pool, m, s, f)


def ffn_buffers(sb, sem, m, tag):
    f = Shared()
    f.first = tag == "in"
    if f.first:
        m.zc = [sb(f"zc_{x}", [2, TILE], F32R) for x in ("hi", "lo")]
        m.hsq = sb("hsq", [2, FC, TILE])
        m.hss = sb("hss", [2, TILE])
        m.scale = sb("scale", [2, 8, BLK])
        m.fz = sb("fz", [2, BLK, P])
        m.fst = sb("fst", [2, BLK, 6])
        m.fmv = sb("fmv", [2, BLK, 2])
        m.raw_tern, m.tern, m.below = m.hsq[:, 1, 0:2, :], m.hsq[:, 0, 0:2, :], m.hsq[:, 0, 2:4, :]
        m.abs_row = sb("abs_row", [2])
        m.thr = sb("thr", [2, 2])
    f.loaded = [sem(f"ffn_{tag}_loaded_{t}") for t in range(NT if f.first else 0)]
    f.stored = sem(f"ffn_{tag}_stored")
    f.turned_x = sem(f"ffn_{tag}_turned_x")
    f.x_in = sem(f"ffn_{tag}_x_in")
    f.stats = sem(f"ffn_{tag}_stats")
    f.mv = sem(f"ffn_{tag}_mv")
    f.var_eps = sem(f"ffn_{tag}_var_eps")
    f.rstd = sem(f"ffn_{tag}_rstd")
    f.sd = sem(f"ffn_{tag}_sd")
    f.sd_rstd = sem(f"ffn_{tag}_sd_rstd")
    f.den = sem(f"ffn_{tag}_den")
    f.part_sums = sem(f"ffn_{tag}_part_sums")
    f.recip = sem(f"ffn_{tag}_recip")
    f.alpha = sem(f"ffn_{tag}_alpha")
    f.z = sem(f"ffn_{tag}_z")
    f.turned_z = sem(f"ffn_{tag}_turned_z")
    f.z_hi = sem(f"ffn_{tag}_z_hi")
    f.z_lo = sem(f"ffn_{tag}_z_lo")
    f.up = sem(f"ffn_{tag}_up")
    f.gelu = sem(f"ffn_{tag}_gelu")
    f.hsq = sem(f"ffn_{tag}_hsq")
    f.hss = sem(f"ffn_{tag}_hss")
    f.ssq = sem(f"ffn_{tag}_ssq")
    f.down = sem(f"ffn_{tag}_down")
    f.ms = sem(f"ffn_{tag}_ms")
    f.rms = sem(f"ffn_{tag}_rms")
    f.rms_eps = sem(f"ffn_{tag}_rms_eps")
    f.rms_recip = sem(f"ffn_{tag}_rms_recip")
    f.beta = sem(f"ffn_{tag}_beta")
    f.x_new = sem(f"ffn_{tag}_x_new")
    f.stats_c = sem(f"ffn_{tag}_stats_c")
    f.mv_c = sem(f"ffn_{tag}_mv_c")
    f.ve_c = sem(f"ffn_{tag}_ve_c")
    f.rstd_c = sem(f"ffn_{tag}_rstd_c")
    f.z_c = sem(f"ffn_{tag}_z_c")
    f.turned_c = sem(f"ffn_{tag}_turned_c")
    return f



def sync_engine(sp, m, s, f, d):
    fin, fout = f
    sp.dma_start(m.ident[:, :], d.ident).then_inc(s.setup_loaded, DMA)
    sp.dma_start(m.x_tm[:, 0, :, :], d.x_rows[0]).then_inc(fin.loaded[0], DMA)
    sp.dma_start(m.raw_tern[:, 0, :].rearrange("p (c d) -> p c d", c=FC),
                 d.w_up.rearrange("(c p) d -> p c d", p=P)).then_inc(s.setup_loaded, DMA)
    sp.dma_start(m.raw_tern[:, 1, :], d.w_down).then_inc(s.setup_loaded, DMA)
    for base, v in d.vectors:
        sp.dma_start(m.par_rows[base:base + LAYERS, :], v).then_inc(s.setup_loaded, DMA)
    sp.dma_start(m.par_rows[B1:NPAR, :], d.b1.rearrange("l (c p) -> (l c) p", p=P)).then_inc(s.setup_loaded, DMA)
    for t in range(1, NT):
        sp.dma_start(m.x_tm[:, t, :, :], d.x_rows[t]).then_inc(fin.loaded[t], DMA)

    def load_weights(pair, i):
        layer = pair * 2 + i
        row = bass.ds(layer, 1)
        if not isinstance(layer, int) or layer > 0:
            wait_apart(sp, s, s.qkv_split, layer)
        for k, w in enumerate(d.kqv):
            sp.dma_start(m.raw_qkv[:, k, :], w[row].rearrange("l p d -> p (l d)")).then_inc(s.raw_qkv_loaded, DMA)
        if not isinstance(layer, int) or layer > 0:
            wait_apart(sp, s, s.w1_split, layer)
        sp.dma_start(m.raw_w1[:, :, :].rearrange("p c d -> p (c d)"),
                     d.W1[row].rearrange("l p d -> p (l d)")).then_inc(s.raw_w1_loaded, DMA)
        if not isinstance(pair, int):
            wait_apart(sp, s, s.proj_o, layer * NT - NT)
        sp.dma_start(m.wo[i][:, :], d.Wo[row].rearrange("l p d -> p (l d)")).then_inc(s.wo_loaded[i], DMA)
        if not isinstance(pair, int):
            wait_apart(sp, s, s.ff_down, layer * NT - NT)
        sp.dma_start(m.w2[i][:, :, :], d.W2[row].rearrange("l p c d -> p (l c) d")).then_inc(s.w2_loaded[i], DMA)

    load_weights(0, 0)
    load_weights(0, 1)
    with sp.Fori(1, PAIRS) as pair:
        load_weights(pair, 0)
        load_weights(pair, 1)
    with sp.Fori(0, NT) as t:
        wait_apart(sp, s, fout.x_new, t + 1)
        sp.dma_start(d.out_rows[bass.ds(t, 1)].rearrange("t p j d -> p (t j) d"),
                     m.x_tm[:, bass.ds(t, 1), :, :].rearrange("p t j d -> p (t j) d")).then_inc(fout.stored, DMA)
    sp.wait_ge(fout.stored, DMA * NT)



def transpose_tile(pe, bank, src, m):
    for j in range(BLK):
        last = pe.transpose(bank[:, j * P:(j + 1) * P], src(j), m.ident[:, :])
    return last


def split_product(pe, bank, w_hi, w_lo, x_hi, x_lo):
    pe.matmul(bank[:, :], w_hi, x_hi, start=True, stop=False)
    pe.matmul(bank[:, :], w_hi, x_lo, start=False, stop=False)
    return pe.matmul(bank[:, :], w_lo, x_hi, start=False, stop=True)


def tensor_engine(pe, m, s, f):
    pe.wait_ge(s.setup_loaded, DMA * 13)
    pe.transpose(m.ps_q[:, 0:NPAR], m.par_rows[0:NPAR, :], m.ident[0:NPAR, 0:NPAR]).then_inc(s.par_turned, 1)
    pe.wait_ge(s.consts, 1)
    pe.wait_ge(s.abs_sums, 2)
    pe.matmul(m.ps_k[:, 0:2], m.ones[:, :], m.abs_row[:, :], start=True, stop=True).then_inc(s.abs_total, 1)
    for w, dst in ((0, m.ps_v), (1, m.ps_o)):
        pe.wait_ge(s.ternary, w + 1)
        for c in range(FC):
            last = pe.transpose(dst[:, c * P:(c + 1) * P], m.tern[:, w, c * P:(c + 1) * P], m.ident[:, :])
        last.then_inc(s.ternary_turned, 1)
    pe.wait_ge(s.setup_kept, 4)

    tensor_ffn(pe, m, s, f[0])
    for tick in range(2 * TICKS):
        tensor_tick(pe, m, s, f, 0, tick)
    with pe.Fori(1, PAIRS) as pair:
        for tick in range(2 * TICKS):
            tensor_tick(pe, m, s, f, pair, tick)
    for tick in range(LAG):
        tensor_tick(pe, m, s, f, PAIRS, tick)
    tensor_ffn(pe, m, s, f[1])


def tensor_tick(pe, m, s, f, pair, tick):
    t, n = tiles_of(pair, tick)

    def project(T, i):
        if not T:
            return
        if T.first:
            pe.wait_ge(s.qkv_split, T.layer + 1)
            if isinstance(T.n, int) and T.n == 1:
                pe.wait_ge(f[0].x_new, NT)
                pe.wait_ge(f[0].ms, NT)
        pe.wait_ge(s.x_split, T.n)
        bank, read, done = ((m.ps_k, s.elu_k, s.proj_k), (m.ps_q, s.elu_q, s.proj_q), (m.ps_v, s.kv_acc, s.proj_v))[i]
        at_least(pe, read, T.n - 1)
        w_hi, w_lo = m.wqkv[T.weights]
        split_product(pe, bank, w_hi[:, i, :], w_lo[:, i, :], m.x_hi[:, T.slot, :], m.x_lo[:, T.slot, :]).then_inc(done, 1)

    def project_o(T, *before):
        if not T:
            return
        if T.first:
            pe.wait_ge(s.wo_loaded[T.weights], T.loads * DMA)
        pe.wait_ge(s.v_ready, T.n)
        bank_left(pe, s.gelu_o, T.n - 1, *before)
        pe.matmul(m.ps_o[:, :], m.wo[T.weights][:, :], m.vf[:, T.par, :], start=True, stop=True).then_inc(s.proj_o, 1)

    def up(T, c):
        if not T:
            return
        if c == 0:
            if T.first:
                pe.wait_ge(s.w1_split, T.layer + 1)
            pe.wait_ge(s.x1_split, T.n)
        at_least(pe, s.gelu_h, T.chunks + (c - 1))
        w_hi, w_lo = m.w1[T.weights]
        split_product(pe, m.ps_h[c % 2], w_hi[:, c, :], w_lo[:, c, :],
                      m.x_hi[:, T.slot, :], m.x_lo[:, T.slot, :]).then_inc(s.ff_up, 1)

    def down(T, c, *before):
        if not T:
            return
        if c == 0:
            if T.first:
                pe.wait_ge(s.w2_loaded[T.weights], T.loads * DMA)
            bank_left(pe, s.gelu_ff, T.n - 1, *before)
        pe.wait_ge(s.gelu_h, T.chunks + (c + 1))
        mm = pe.matmul(m.ps_o[:, :], m.w2[T.weights][:, c, :], m.h[:, T.par, c, :], start=c == 0, stop=c == FC - 1)
        if c == FC - 1:
            mm.then_inc(s.ff_down, 1)

    def turn_y(T, i, *before):
        if not T:
            return
        pe.wait_ge((s.y1, s.y2)[i], T.n)
        bank_left(pe, (s.z1, s.z2)[i], T.n - 1, *before)
        y = m.y[i][:, T.par, :]
        transpose_tile(pe, m.ps_ty, lambda j: y[:, j * P:(j + 1) * P], m).then_inc((s.turned_y1, s.turned_y2)[i], 1)

    def turn_z(T, i, *before):
        if not T:
            return
        pe.wait_ge((s.z1, s.z2)[i], T.n)
        bank_left(pe, (s.x1_full, s.x_full)[i], T.n - 1 + (0, NT)[i], *before)
        transpose_tile(pe, m.ps_tz, lambda j: m.z[i][:, T.par, j, :], m).then_inc((s.turned_z1, s.turned_z2)[i], 1)

    up(t(1, 3), 2)
    turn_y(t(0, 3), 1, s.z1, n(0, 2))
    turn_z(t(0, 2), 0, s.x_full, n(1, 4) + NT)
    up(t(1, 3), 3)
    project(t(0, 0), KEY)
    project(t(0, 0), QUERY)
    down(t(1, 3), 0, s.gelu_o, n(1, 2))
    down(t(1, 3), 1)
    turn_y(t(1, 2), 0, s.z2, n(0, 3))
    down(t(1, 3), 2)
    down(t(1, 3), 3)
    turn_z(t(0, 3), 1, s.x1_full, n(0, 2))
    up(t(0, 2), 0)
    project(t(0, 0), VALUE)
    up(t(0, 2), 1)
    project_o(t(0, 1), s.gelu_ff, n(1, 3))
    up(t(0, 2), 2)
    turn_y(t(1, 3), 1, s.z1, n(1, 2))
    turn_z(t(1, 2), 0, s.x_full, n(0, 3) + NT)
    up(t(0, 2), 3)
    project(t(1, 0), KEY)
    down(t(0, 2), 0, s.gelu_o, n(0, 1))
    down(t(0, 2), 1)
    project(t(1, 0), QUERY)
    turn_y(t(0, 1), 0, s.z2, n(1, 3))
    down(t(0, 2), 2)
    down(t(0, 2), 3)
    up(t(1, 2), 0)
    project(t(1, 0), VALUE)
    turn_z(t(1, 3), 1, s.x1_full, n(1, 2))
    up(t(1, 2), 1)
    project_o(t(1, 1), s.gelu_ff, n(0, 2))


def tensor_ffn(pe, m, s, f):
    ps_down = (m.ps_q, m.ps_o)

    def enter(t):
        if not 0 <= t < NT:
            return
        pe.wait_ge(s.x_full, LAYERS * NT + t + 1)
        at_least(pe, f.x_in, t)
        transpose_tile(pe, m.ps_k, lambda j: m.x_fm[:, t, j * P:(j + 1) * P], m).then_inc(f.turned_x, 1)

    def turn(t):
        if not 0 <= t < NT:
            return
        pe.wait_ge(f.z, t + 1)
        at_least(pe, f.z_lo, t)
        if t == 0 and not f.first:
            pe.wait_ge(s.z2, LAYERS * NT)
            pe.wait_ge(s.gelu_h, LAYERS * NT * FC)
        transpose_tile(pe, m.ps_ty, lambda j: m.fz[:, t % 2, j, :], m).then_inc(f.turned_z, 1)

    def up(t, c):
        if not 0 <= t < NT:
            return
        if c == 0:
            pe.wait_ge(f.z_lo, t + 1)
        at_least(pe, f.gelu, FC * t + c - 1)
        pe.matmul(m.ps_h[c % 2][:, :], m.upT[:, c, :], m.zc[0][:, t % 2, :], start=True, stop=False)
        pe.matmul(m.ps_h[c % 2][:, :], m.upT[:, c, :], m.zc[1][:, t % 2, :], start=False, stop=True).then_inc(f.up, 1)

    def down(t):
        if not 0 <= t < NT:
            return
        at_least(pe, f.x_new, t - 1)
        if t == 0 and not f.first:
            pe.wait_ge(s.gelu_ff, LAYERS * NT)
            pe.wait_ge(s.elu_q, LAYERS * NT)
        pe.wait_ge(f.gelu, FC * (t + 1))
        for j in range(BLK):
            for c in range(FC):
                last = pe.matmul(ps_down[t % 2][:, j * P:(j + 1) * P], m.h[:, t % 2, c, j * P:(j + 1) * P],
                                 m.downT[:, c, :], start=c == 0, stop=c == FC - 1)
        last.then_inc(f.down, 1)

    def squares(t):
        if not 0 <= t < NT:
            return
        pe.wait_ge(f.hss, t + 1)
        at_least(pe, f.ms, t)
        for j in range(BLK):
            last = pe.matmul(m.ps_v[:, j:j + 1], m.hss[:, t % 2, j * P:(j + 1) * P], m.ones[:, 0:1],
                             start=True, stop=True)
        last.then_inc(f.ssq, 1)

    def turn_c(t):
        if not 0 <= t < NT:
            return
        pe.wait_ge(f.z_c, t + 1)
        at_least(pe, s.x_hi, t)
        transpose_tile(pe, m.ps_tz, lambda j: m.z[0][:, t % 2, j, :], m).then_inc(f.turned_c, 1)

    for tick in range(NT + (10 if f.first else 6)):
        if f.first:
            up(tick - 1, 0)
            up(tick - 1, 1)
            turn(tick - 0)
            squares(tick - 3)
            up(tick - 1, 2)
            up(tick - 1, 3)
            turn_c(tick - 7)
            down(tick - 2)
        else:
            up(tick - 5, 2)
            turn(tick - 4)
            up(tick - 5, 3)
            down(tick - 6)
            up(tick - 4, 0)
            up(tick - 4, 1)
            squares(tick - 6)
            enter(tick - 0)



def scalar_engine(act, m, s, f):
    scalar_ffn(act, m, s, f[0])
    for tick in range(2 * TICKS):
        scalar_tick(act, m, s, 0, tick)
    with act.Fori(1, PAIRS) as pair:
        for tick in range(2 * TICKS):
            scalar_tick(act, m, s, pair, tick)
    for tick in range(LAG):
        scalar_tick(act, m, s, PAIRS, tick)
    scalar_ffn(act, m, s, f[1])


def scalar_tick(act, m, s, pair, tick):
    t, n = tiles_of(pair, tick)

    def negative(T, i):
        if not T:
            return
        e, bank, base, proj, done = ((m.e_k, m.ps_k, NEG_BK, s.proj_k, s.neg_k), (m.e_q, m.ps_q, NEG_BQ, s.proj_q, s.neg_q))[i]
        wait_apart(act, s, proj, T.n)
        act.activation(e[:, T.par, :], bank[:, :], ACT.Relu, bias=column(m, base, T.layer), scale=-1.0).then_inc(done, 1)

    def exp(T, i):
        if not T:
            return
        e, neg, done = ((m.e_k, s.neg_k, s.exp_k), (m.e_q, s.neg_q, s.exp_q))[i]
        wait_apart(act, s, neg, T.n)
        act.activation(e[:, T.par, :], e[:, T.par, :], ACT.Exp, scale=-1.0).then_inc(done, 1)

    def sum_k(T):
        if not T:
            return
        wait_apart(act, s, s.elu_k, T.n)
        for b in range(2):
            cols = slice(b * SEQ, (b + 1) * SEQ)
            last = act.activation(m.kf[:, T.par, cols], m.elu_k[:, T.par, cols], ACT.Identity, bias=1.0,
                                  accum_out=m.ksum[:, T.par, b:b + 1])
        last.then_inc(s.ksum, 1)

    def log_den(T):
        if not T:
            return
        wait_apart(act, s, s.den_ready, T.n)
        act.activation(m.rec[:, T.par, :], m.den[:, T.par, :], ACT.Ln, bias=m.eps[:, 0:1]).then_inc(s.log_den, 1)

    def recip(T):
        if not T:
            return
        wait_apart(act, s, s.log_den, T.n)
        act.activation(m.rec[:, T.par, :], m.rec[:, T.par, :], ACT.Exp, scale=-1.0).then_inc(s.recip, 1)

    def gelu(bank, ready, n, dst, bias, done):
        wait_apart(act, s, ready, n)
        act.activation(dst, bank[:, :], ACT.Gelu_apprx_tanh, bias=bias).then_inc(done, 1)

    def gelu_o(T):
        if T:
            gelu(m.ps_o, s.proj_o, T.n, m.y[0][:, T.par, :], column(m, BO, T.layer), s.gelu_o)

    def gelu_h(T, c):
        if T:
            gelu(m.ps_h[c % 2], s.ff_up, T.chunks + (c + 1), m.h[:, T.par, c, :],
                 column(m, B1, T.layer, c, FC), s.gelu_h)

    def gelu_ff(T):
        if T:
            gelu(m.ps_o, s.ff_down, T.n, m.y[1][:, T.par, :], column(m, B2, T.layer), s.gelu_ff)

    def full(T, i):
        if not T:
            return
        wait_apart(act, s, (s.turned_z1, s.turned_z2)[i], T.n)
        act.activation(m.x_fm[:, T.slot, :], m.ps_tz[:, :], ACT.Identity,
                       bias=column(m, (LN1B, LN2B)[i], T.layer),
                       scale=column(m, (LN1S, LN2S)[i], T.layer)).then_inc((s.x1_full, s.x_full)[i], 1)

    exp(t(0, 1), KEY)
    exp(t(0, 1), QUERY)
    gelu_ff(t(1, 4))
    gelu_h(t(0, 3), 0)
    gelu_h(t(0, 3), 1)
    sum_k(t(0, 1))
    full(t(0, 4), 1)
    gelu_h(t(0, 3), 2)
    gelu_o(t(0, 2))
    full(t(1, 3), 0)
    gelu_h(t(0, 3), 3)
    negative(t(1, 1), KEY)
    act.preload_act_table_set(EXP_AND_LN)
    log_den(t(0, 1))
    negative(t(1, 1), QUERY)
    exp(t(1, 1), KEY)
    recip(t(0, 1))
    exp(t(1, 1), QUERY)
    gelu_ff(t(0, 3))
    gelu_h(t(1, 3), 0)
    full(t(1, 4), 1)
    sum_k(t(1, 1))
    gelu_h(t(1, 3), 1)
    gelu_o(t(1, 2))
    gelu_h(t(1, 3), 2)
    full(t(0, 2), 0)
    gelu_h(t(1, 3), 3)
    act.preload_act_table_set(EXP_AND_LN)
    log_den(t(1, 1))
    negative(t(0, 0), KEY)
    recip(t(1, 1))
    negative(t(0, 0), QUERY)


def scalar_ffn(act, m, s, f):
    def z_hi(t):
        if not 0 <= t < NT:
            return
        act.wait_ge(f.turned_z, t + 1)
        at_least(act, f.up, FC * (t - 1))
        act.activation(m.zc[0][:, t % 2, :], m.ps_ty[:, :], ACT.Copy).then_inc(f.z_hi, 1)

    def gelu(t, c):
        if not 0 <= t < NT:
            return
        act.wait_ge(f.up, FC * t + c + 1)
        if c == 0:
            at_least(act, f.down, t - 1)
        act.activation(m.h[:, t % 2, c, :], m.ps_h[c % 2][:, :], ACT.Gelu).then_inc(f.gelu, 1)

    def square(t):
        if not 0 <= t < NT:
            return
        act.wait_ge(f.gelu, FC * (t + 1))
        at_least(act, f.hss, t - 1)
        act.activation(m.hsq[:, t % 2, :, :], m.h[:, t % 2, :, :], ACT.Square).then_inc(f.hsq, 1)

    def full(t):
        if not 0 <= t < NT:
            return
        act.wait_ge(f.turned_c, t + 1)
        act.activation(m.x_fm[:, t, :], m.ps_tz[:, :], ACT.Copy).then_inc(s.x_full, 1)

    def hi(t):
        if not 0 <= t < NT:
            return
        act.wait_ge(f.turned_c, t + 1)
        act.activation(m.x_hi[:, t, :], m.ps_tz[:, :], ACT.Copy).then_inc(s.x_hi, 1)

    for tick in range(NT + (10 if f.first else 6)):
        if f.first:
            gelu(tick - 2, 2)
            gelu(tick - 2, 3)
            square(tick - 2)
            gelu(tick - 1, 0)
            gelu(tick - 1, 1)
            z_hi(tick - 0)
            full(tick - 8)
            hi(tick - 8)
        else:
            square(tick - 2)
            gelu(tick - 1, 0)
            gelu(tick - 1, 1)
            gelu(tick - 1, 2)
            z_hi(tick - 0)
            gelu(tick - 1, 3)



def block_stats(dve, src, st, done):
    for j in range(BLK):
        last = dve.bn_stats(st[:, j, :], src(j))
    last.then_inc(done, 1)


def block_means(dve, s, st, mv, ready, n, done):
    wait_apart(dve, s, ready, n)
    for j in range(BLK):
        last = dve.bn_aggr(mv[:, j, :], st[:, j, :])
    last.then_inc(done, 1)


def normalise(dve, dst, src, mv, scale, done):
    for j in range(BLK):
        last = dve.tensor_scalar(dst[:, j, :], src(j), mv[:, j, 0:1], scale[:, j:j + 1], ALU.subtract, ALU.mult)
    last.then_inc(done, 1)


def vector_engine(dve, m, s, f):
    dve.wait_ge(s.setup_loaded, DMA * 13)
    for w in range(2):
        dve.tensor_reduce(m.abs_row[:, w:w + 1], m.raw_tern[:, w, :], AX_X, ALU.add,
                          apply_absolute_value=True).then_inc(s.abs_sums, 1)
    dve.wait_ge(s.abs_total, 1)
    for i, half in enumerate((0.5, -0.5)):
        dve.tensor_scalar(m.thr[:, i, :], m.ps_k[:, 0:2], 1.0 / (FF * P), half, ALU.mult,
                          ALU.mult).then_inc(s.thresholds, 1)
    dve.wait_ge(s.thresholds, 2)
    for w in range(2):
        dve.tensor_scalar(m.below[:, w, :], m.raw_tern[:, w, :], m.thr[:, 1, w:w + 1], None,
                          ALU.is_lt).then_inc(s.above, 1)
    for w in range(2):
        dve.wait_ge(s.above, w + 1)
        dve.scalar_tensor_tensor(m.tern[:, w, :], m.raw_tern[:, w, :], m.thr[:, 0, w:w + 1], m.below[:, w, :],
                                 ALU.is_gt, ALU.subtract).then_inc(s.ternary, 1)
    dve.wait_ge(s.par_turned, 1)
    dve.tensor_copy(m.par[:, 0:NPAR], m.ps_q[:, 0:NPAR]).then_inc(s.setup_kept, 1)
    for w, dst, bank in ((0, m.upT, m.ps_v), (1, m.downT, m.ps_o)):
        dve.wait_ge(s.ternary_turned, w + 1)
        dve.tensor_copy(dst[:, :, :].rearrange("p c d -> p (c d)"), bank[:, :]).then_inc(s.setup_kept, 1)

    dve.wait_ge(s.setup_kept, 1)
    dve.tensor_scalar(m.par[:, NEG_BQ:NEG_BK + LAYERS], m.par[:, BQ:BK + LAYERS], -1.0, None,
                      ALU.mult).then_inc(s.setup_kept, 1)

    vector_ffn(dve, m, s, f[0])
    for tick in range(2 * TICKS):
        vector_tick(dve, m, s, 0, tick)
    with dve.Fori(1, PAIRS) as pair:
        for tick in range(2 * TICKS):
            vector_tick(dve, m, s, pair, tick)
    for tick in range(LAG):
        vector_tick(dve, m, s, PAIRS, tick)
    vector_ffn(dve, m, s, f[1])


def vector_tick(dve, m, s, pair, tick):
    t, n = tiles_of(pair, tick)

    def minus_one(T, i):
        if not T:
            return
        e, exp, done = ((m.e_k, s.exp_k, s.expm1_k), (m.e_q, s.exp_q, s.expm1_q))[i]
        dve.wait_ge(exp, T.n)
        dve.tensor_scalar(e[:, T.par, :], e[:, T.par, :], 1.0, None, ALU.subtract).then_inc(done, 1)

    def elu(T, i):
        if not T:
            return
        e, bank, dst, base, expm1, done = ((m.e_k, m.ps_k, m.elu_k, BK, s.expm1_k, s.elu_k),
                                           (m.e_q, m.ps_q, m.elu_q, BQ, s.expm1_q, s.elu_q))[i]
        at_least(dve, s.num_ready, T.n - 2)
        dve.wait_ge(expm1, T.n)
        dve.scalar_tensor_tensor(dst[:, T.par, :], bank[:, :], column(m, base, T.layer), e[:, T.par, :],
                                 ALU.add, ALU.max).then_inc(done, 1)

    def sum_kv(T):
        if not T:
            return
        dve.wait_ge(s.elu_k, T.n)
        dve.wait_ge(s.proj_v, T.n)
        for b in range(2):
            cols = slice(b * SEQ, (b + 1) * SEQ)
            last = dve.scalar_tensor_tensor(m.kvf[:, T.par, cols], m.elu_k[:, T.par, cols], 1.0, m.ps_v[:, cols],
                                            ALU.add, ALU.mult, accum_out=m.kvacc[:, T.par, b:b + 1])
        last.then_inc(s.kv_acc, 1)

    def kv(T):
        if not T:
            return
        dve.wait_ge(s.ksum, T.n)
        dve.wait_ge(s.kv_acc, T.n)
        dve.scalar_tensor_tensor(m.kv[:, T.par, :], m.ksum[:, T.par, :], column(m, BV, T.layer),
                                 m.kvacc[:, T.par, :], ALU.mult, ALU.add).then_inc(s.kv_ready, 1)

    def newton_a(T):
        if not T:
            return
        dve.wait_ge(s.recip, T.n)
        dve.scalar_tensor_tensor(m.nwt[:, T.par, :], m.den[:, T.par, :], EPS_ATTN, m.rec[:, T.par, :],
                                 ALU.add, ALU.mult).then_inc(s.newton_a, 1)

    def newton_c(T):
        if not T:
            return
        dve.wait_ge(s.newton_a, T.n)
        dve.scalar_tensor_tensor(m.rec[:, T.par, :], m.nwt[:, T.par, :], 2.0, m.rec[:, T.par, :],
                                 ALU.subtract, ALU.mult).then_inc(s.newton_c, 1)

    def newton_v(T):
        if not T:
            return
        dve.wait_ge(s.num_ready, T.n)
        dve.wait_ge(s.newton_c, T.n)
        dve.scalar_tensor_tensor(m.vf[:, T.par, :], m.num[:, T.par, :], -1.0, m.rec[:, T.par, :],
                                 ALU.mult, ALU.mult).then_inc(s.v_ready, 1)

    def source(j):
        return m.ps_ty[:, j * P:(j + 1) * P]

    def stats(T, i):
        if not T:
            return
        dve.wait_ge((s.turned_y1, s.turned_y2)[i], T.n)
        block_stats(dve, source, m.st[i][:, T.par], (s.stats1, s.stats2)[i])
        block_means(dve, s, m.st[i][:, T.par], m.mv[i][:, T.par], (s.stats1, s.stats2)[i], T.n, (s.mv1, s.mv2)[i])

    def z(T, i):
        if not T:
            return
        dve.wait_ge((s.rstd1, s.rstd2)[i], T.n)
        normalise(dve, m.z[i][:, T.par], source, m.mv[i][:, T.par], m.rstd[i][:, T.par], (s.z1, s.z2)[i])

    def hi(T, i):
        if not T:
            return
        full, done, more = ((s.x1_full, s.x1_hi, 0), (s.x_full, s.x_hi, NT))[i]
        dve.wait_ge(full, T.n + more)
        dve.tensor_copy(m.x_hi[:, T.slot, :], m.x_fm[:, T.slot, :]).then_inc(done, 1)

    z(t(0, 2), 0)
    hi(t(1, 4), 1)
    stats(t(0, 3), 1)
    sum_kv(t(1, 1))
    newton_c(t(0, 1))
    z(t(0, 3), 1)
    hi(t(0, 2), 0)
    kv(t(1, 1))
    newton_v(t(0, 1))
    stats(t(1, 2), 0)
    newton_a(t(1, 1))
    minus_one(t(0, 0), KEY)
    newton_c(t(1, 1))
    elu(t(0, 0), KEY)
    minus_one(t(0, 0), QUERY)
    z(t(1, 2), 0)
    elu(t(0, 0), QUERY)
    stats(t(1, 3), 1)
    sum_kv(t(0, 0))
    hi(t(1, 2), 0)
    hi(t(0, 3), 1)
    z(t(1, 3), 1)
    newton_v(t(1, 1))
    stats(t(0, 1), 0)
    minus_one(t(1, 0), KEY)
    kv(t(0, 0))
    newton_a(t(0, 0))
    minus_one(t(1, 0), QUERY)
    elu(t(1, 0), KEY)
    elu(t(1, 0), QUERY)


def vector_ffn(dve, m, s, f):
    eps_var, rstd, sd, den, recip, alpha, ms, beta = range(8)

    def source(t):
        return lambda j: m.x_tm[:, t, j, :]

    def x_in(t):
        if not 0 <= t < NT:
            return
        dve.wait_ge(f.turned_x, t + 1)
        x = m.x_tm[:, t, :, :].rearrange("p j d -> p (j d)")
        dve.tensor_tensor(x, m.ps_k[:, :], x, ALU.add).then_inc(f.x_in, 1)

    def enter_stats(t):
        if not 0 <= t < NT:
            return
        if f.first:
            dve.wait_ge(f.loaded[t], DMA)
        else:
            dve.wait_ge(f.x_in, t + 1)
        block_stats(dve, source(t), m.fst[:, t % 2], f.stats)
        block_means(dve, s, m.fst[:, t % 2], m.fmv[:, t % 2], f.stats, t + 1, f.mv)
        dve.wait_ge(f.mv, t + 1)
        dve.tensor_scalar(m.scale[:, t % 2, eps_var, :], m.fmv[:, t % 2, :, 1], EPS_OUTER, None,
                          ALU.add).then_inc(f.var_eps, 1)

    def alpha_(t):
        if not 0 <= t < NT:
            return
        sc = m.scale[:, t % 2]
        dve.wait_ge(f.sd, t + 1)
        dve.wait_ge(f.rstd, t + 1)
        dve.tensor_tensor(sc[:, sd, :], sc[:, sd, :], sc[:, rstd, :], ALU.mult).then_inc(f.sd_rstd, 1)
        dve.wait_ge(f.sd_rstd, t + 1)
        dve.tensor_scalar(sc[:, den, :], sc[:, sd, :], EPS_RMS, None, ALU.add).then_inc(f.den, 1)
        dve.wait_ge(f.den, t + 1)
        dve.reciprocal(sc[:, recip, :], sc[:, den, :]).then_inc(f.recip, 1)
        dve.wait_ge(f.recip, t + 1)
        dve.tensor_tensor(sc[:, alpha, :], sc[:, recip, :], sc[:, rstd, :], ALU.mult).then_inc(f.alpha, 1)

    def normal(t):
        if not 0 <= t < NT:
            return
        dve.wait_ge(f.alpha, t + 1)
        at_least(dve, f.turned_z, t - 1)
        normalise(dve, m.fz[:, t % 2], source(t), m.fmv[:, t % 2], m.scale[:, t % 2, alpha, :], f.z)

    def low(t):
        if not 0 <= t < NT:
            return
        dve.wait_ge(f.z_hi, t + 1)
        dve.tensor_tensor(m.zc[1][:, t % 2, :], m.ps_ty[:, :], m.zc[0][:, t % 2, :].bitcast(F32),
                          ALU.subtract).then_inc(f.z_lo, 1)

    def mean_square(t):
        if not 0 <= t < NT:
            return
        dve.wait_ge(f.ssq, t + 1)
        dve.tensor_scalar(m.scale[:, t % 2, ms, :], m.ps_v[:, 0:BLK], 1.0 / FF, None, ALU.mult).then_inc(f.ms, 1)

    def beta_(t):
        if not 0 <= t < NT:
            return
        sc = m.scale[:, t % 2]
        dve.wait_ge(f.rms, t + 1)
        dve.tensor_scalar(sc[:, ms, :], sc[:, ms, :], EPS_RMS, None, ALU.add).then_inc(f.rms_eps, 1)
        dve.wait_ge(f.rms_eps, t + 1)
        dve.reciprocal(sc[:, ms, :], sc[:, ms, :]).then_inc(f.rms_recip, 1)
        dve.wait_ge(f.rms_recip, t + 1)
        dve.tensor_scalar(sc[:, beta, :], sc[:, ms, :], 0.5, None, ALU.mult).then_inc(f.beta, 1)

    def residual(t):
        if not 0 <= t < NT:
            return
        sc = m.scale[:, t % 2]
        dve.wait_ge(f.beta, t + 1)
        dve.wait_ge(f.down, t + 1)
        bank = (m.ps_q, m.ps_o)[t % 2]
        for j in range(BLK):
            last = dve.scalar_tensor_tensor(m.x_tm[:, t, j, :], bank[:, j * P:(j + 1) * P], sc[:, beta, j:j + 1],
                                            m.x_tm[:, t, j, :], ALU.mult, ALU.add)
        last.then_inc(f.x_new, 1)

    def stats_c(t):
        if not 0 <= t < NT:
            return
        dve.wait_ge(f.x_new, t + 1)
        block_stats(dve, source(t), m.st[0][:, t % 2], f.stats_c)
        block_means(dve, s, m.st[0][:, t % 2], m.mv[0][:, t % 2], f.stats_c, t + 1, f.mv_c)
        dve.wait_ge(f.mv_c, t + 1)
        dve.tensor_scalar(m.ve[0][:, t % 2, :], m.mv[0][:, t % 2, :, 1], EPS_OUTER, None, ALU.add).then_inc(f.ve_c, 1)

    def z_c(t):
        if not 0 <= t < NT:
            return
        dve.wait_ge(f.rstd_c, t + 1)
        at_least(dve, f.turned_c, t - 1)
        normalise(dve, m.z[0][:, t % 2], source(t), m.mv[0][:, t % 2], m.rstd[0][:, t % 2], f.z_c)

    for tick in range(NT + (10 if f.first else 6)):
        if f.first:
            enter_stats(tick - 0)
            residual(tick - 6)
            low(tick - 2)
            alpha_(tick - 1)
            mean_square(tick - 5)
            stats_c(tick - 6)
            normal(tick - 1)
            beta_(tick - 5)
            z_c(tick - 7)
        else:
            mean_square(tick - 6)
            enter_stats(tick - 1)
            beta_(tick - 6)
            low(tick - 3)
            residual(tick - 6)
            alpha_(tick - 2)
            x_in(tick - 0)
            normal(tick - 2)



def gpsimd_engine(pool, m, s, f):
    pool.memset(m.ones[:, :], 1.0)
    pool.memset(m.eps[:, :], EPS_ATTN)
    pool.memset(m.minus_half[:, :], -0.5)
    pool.memset(m.plus_half[:, :], 0.5).then_inc(s.consts, 1)
    pool.wait_ge(s.consts, 1)
    gpsimd_ffn(pool, m, s, f[0], lambda: (split_qkv(pool, m, s, 0, 0), split_w1(pool, m, s, 0, 0)))
    for tick in range(2 * TICKS - 3):
        gpsimd_tick(pool, m, s, 0, tick)
    with pool.Fori(1, PAIRS) as pair:
        for tick in range(-3, 2 * TICKS - 3):
            gpsimd_tick(pool, m, s, pair, tick)
    for tick in range(-3, LAG):
        gpsimd_tick(pool, m, s, PAIRS, tick)
    gpsimd_ffn(pool, m, s, f[1], None)


def split(pool, m, s, layer, raw, pair, loaded, count, hi, done, used, uses):
    wait_apart(pool, s, loaded, count)
    if not isinstance(layer, int):
        wait_apart(pool, s, used, uses)
    pool.tensor_copy(pair[0][:, :, :], raw[:, :, :]).then_inc(hi, 1)
    wait_apart(pool, s, hi, layer + 1)
    pool.tensor_tensor(pair[1][:, :, :], raw[:, :, :], pair[0][:, :, :].bitcast(F32), ALU.subtract).then_inc(done, 1)


def split_qkv(pool, m, s, layer, i):
    split(pool, m, s, layer, m.raw_qkv, m.wqkv[i], s.raw_qkv_loaded, layer * (3 * DMA) + 3 * DMA, s.raw_qkv_hi,
          s.qkv_split, s.proj_v, layer * NT - NT)


def split_w1(pool, m, s, layer, i):
    split(pool, m, s, layer, m.raw_w1, m.w1[i], s.raw_w1_loaded, layer * DMA + DMA, s.raw_w1_hi, s.w1_split,
          s.ff_down, layer * NT - NT)


def inverse_root(pool, m, s, dst, tmp, var, eps, ready, n, mid, done):
    wait_apart(pool, s, ready, n)
    pool.tensor_scalar(tmp, var, eps, None, ALU.add).then_inc(mid, 1)
    wait_apart(pool, s, mid, n)
    pool.tensor_tensor(dst, tmp, m.minus_half[:, :], ALU.pow).then_inc(done, 1)


def gpsimd_tick(pool, m, s, pair, tick):
    t, n = tiles_of(pair, tick)

    def add_residual(T, i):
        if not T:
            return
        wait_apart(pool, s, (s.gelu_o, s.gelu_ff)[i], T.n)
        y = m.y[i][:, T.par, :]
        pool.tensor_tensor(y, y, m.x_fm[:, T.slot, :], ALU.add).then_inc((s.y1, s.y2)[i], 1)

    def rstd(T, i):
        if not T:
            return
        inverse_root(pool, m, s, m.rstd[i][:, T.par, :], m.ve[i][:, T.par, :], m.mv[i][:, T.par, :, 1], EPS_LN,
                     (s.mv1, s.mv2)[i], T.n, (s.ve1, s.ve2)[i], (s.rstd1, s.rstd2)[i])

    def low(T, i):
        if not T:
            return
        hi, done, more = ((s.x1_hi, s.x1_split, 0), (s.x_hi, s.x_split, NT))[i]
        wait_apart(pool, s, hi, T.n + more)
        pool.tensor_tensor(m.x_lo[:, T.slot, :], m.x_fm[:, T.slot, :], m.x_hi[:, T.slot, :].bitcast(F32),
                           ALU.subtract).then_inc(done, 1)

    def scaled_q(T, sums, dst, ready, done):
        wait_apart(pool, s, s.elu_q, T.n)
        wait_apart(pool, s, ready, T.n)
        for b in range(2):
            cols = slice(b * SEQ, (b + 1) * SEQ)
            last = pool.tensor_scalar(dst[:, T.par, cols], m.elu_q[:, T.par, cols], 1.0, sums[:, T.par, b:b + 1],
                                      ALU.add, ALU.mult)
        last.then_inc(done, 1)

    def den(T):
        if T:
            scaled_q(T, m.ksum, m.den, s.ksum, s.den_ready)

    def num(T):
        if T:
            scaled_q(T, m.kv, m.num, s.kv_ready, s.num_ready)

    den(t(1, 1))
    rstd(t(0, 3), 1)
    add_residual(t(1, 2), 0)
    low(t(1, 4), 1)
    low(t(0, 2), 0)
    num(t(1, 1))
    rstd(t(1, 2), 0)
    add_residual(t(1, 3), 1)
    den(t(0, 0))
    rstd(t(1, 3), 1)
    add_residual(t(0, 1), 0)
    low(t(0, 3), 1)
    low(t(1, 2), 0)
    rstd(t(0, 1), 0)
    add_residual(t(0, 2), 1)
    num(t(0, 0))
    layer, i = pair * 2 + (tick // TICKS + 1), (tick // TICKS + 1) % 2
    if not isinstance(pair, int) or layer < LAYERS:
        if tick % TICKS == 1:
            split_qkv(pool, m, s, layer, i)
        if tick % TICKS == 3:
            split_w1(pool, m, s, layer, i)


def gpsimd_ffn(pool, m, s, f, split_first_weights):
    eps_var, rstd_, sd_, den, recip, alpha, ms, beta = range(8)

    def rstd(t):
        if not 0 <= t < NT:
            return
        pool.wait_ge(f.var_eps, t + 1)
        at_least(pool, f.alpha, t - 1)
        pool.tensor_tensor(m.scale[:, t % 2, rstd_, :], m.scale[:, t % 2, eps_var, :], m.minus_half[:, :],
                           ALU.pow).then_inc(f.rstd, 1)

    def sd(t):
        if not 0 <= t < NT:
            return
        pool.wait_ge(f.mv, t + 1)
        at_least(pool, f.alpha, t - 1)
        pool.tensor_tensor(m.scale[:, t % 2, sd_, :], m.fmv[:, t % 2, :, 1], m.plus_half[:, :],
                           ALU.pow).then_inc(f.sd, 1)

    def sum_squares(t):
        if not 0 <= t < NT:
            return
        pool.wait_ge(f.hsq, t + 1)
        sq, total = m.hsq[:, t % 2, :, :], m.hss[:, t % 2, :]
        at_least(pool, f.ssq, t - 1)
        pool.tensor_tensor(total, sq[:, 0, :], sq[:, 1, :], ALU.add).then_inc(f.part_sums, 1)
        pool.wait_ge(f.part_sums, 2 * t + 1)
        pool.tensor_tensor(total, total, sq[:, 2, :], ALU.add).then_inc(f.part_sums, 1)
        pool.wait_ge(f.part_sums, 2 * t + 2)
        pool.tensor_tensor(total, total, sq[:, 3, :], ALU.add).then_inc(f.hss, 1)

    def rms(t):
        if not 0 <= t < NT:
            return
        sc = m.scale[:, t % 2]
        pool.wait_ge(f.ms, t + 1)
        pool.tensor_tensor(sc[:, ms, :], sc[:, ms, :], m.plus_half[:, :], ALU.pow).then_inc(f.rms, 1)

    def rstd_c(t):
        if not 0 <= t < NT:
            return
        pool.wait_ge(f.ve_c, t + 1)
        at_least(pool, f.z_c, t - 1)
        pool.tensor_tensor(m.rstd[0][:, t % 2, :], m.ve[0][:, t % 2, :], m.minus_half[:, :],
                           ALU.pow).then_inc(f.rstd_c, 1)

    def x_low(t):
        if not 0 <= t < NT:
            return
        pool.wait_ge(s.x_hi, t + 1)
        pool.wait_ge(s.x_full, t + 1)
        pool.tensor_tensor(m.x_lo[:, t, :], m.x_fm[:, t, :], m.x_hi[:, t, :].bitcast(F32),
                           ALU.subtract).then_inc(s.x_split, 1)

    for tick in range(NT + (10 if f.first else 6)):
        if f.first:
            if tick == NT:
                split_first_weights()
            rstd(tick - 1)
            rstd_c(tick - 7)
            sum_squares(tick - 4)
            rms(tick - 5)
            sd(tick - 0)
            x_low(tick - 10)
        else:
            sd(tick - 1)
            rstd(tick - 0)
            sum_squares(tick - 3)
            rms(tick - 4)


_INS = ["x", "Wq", "bq", "Wk", "bk", "Wv", "bv", "Wo", "bo", "ln1_s", "ln1_b", "W1", "b1", "W2", "b2",
        "ln2_s", "ln2_b"]
_FFN = ["w_up", "w_down"]


def kernel(**inputs):
    import numpy as np
    import concourse.bacc as bacc
    from concourse.bass_utils import run_bass_kernel_spmd

    nc = bacc.Bacc("TRN2", target_bir_lowering=False, num_devices=1)
    given = [(n, inputs[f"L0_attn_{n}"]) for n in _INS] + [(n, inputs[f"L0_ffn_{n}"]) for n in _FFN]
    given.append(("identity", np.eye(P, dtype=np.float32)))
    arrays, args = {}, []
    for name, value in given:
        a = np.ascontiguousarray(value)
        arrays[f"in_{name}"] = a
        args.append(nc.dram_tensor(f"in_{name}", a.shape, mybir.dt.from_np(a.dtype), kind="ExternalInput").ap())
    x = arrays["in_x"]
    args.append(nc.dram_tensor("out_0", x.shape, F32, kind="ExternalOutput").ap())
    macaron(nc, *args)
    return run_bass_kernel_spmd(nc, [arrays], core_ids=[0]).results[0]["out_0"]
```

```python
from contextlib import ExitStack

import concourse.bass as bass
from concourse import mybir

P = 128
LAYERS = 8
SEQ = 256
TILE = 2 * SEQ
NT = 8
BLK = TILE // P
FC = 4
FF = FC * P
PAIRS = LAYERS // 2
TICKS = NT // 2
LAG = 4
POOL_START = -3
KEY, QUERY, VALUE = 0, 1, 2
EXP_AND_LN = "natural_log_exp_and_others"

EPS_ATTN = 1e-6
EPS_LN = 1e-6
EPS_OUTER = 1e-5
EPS_RMS = 1e-8

F32 = mybir.dt.float32
F32R = mybir.dt.float32r
ALU = mybir.AluOpType
ACT = mybir.ActivationFunctionType
AX_X = mybir.AxisListType.X

BQ, BK, BV, BO, LN1S, LN1B, B2, LN2S, LN2B, B1 = (LAYERS * k for k in range(10))
NPAR = B1 + FC * LAYERS
NEG_BQ, NEG_BK = NPAR, NPAR + LAYERS
DMA = 16


class Shared:
    pass


class Tile:

    def __init__(self, pair, rel):
        self.n = pair * (2 * NT) + (rel + 1)
        self.layer = pair * 2 + rel // NT
        self.weights = (rel // NT) % 2
        self.loads = pair + (rel // (2 * NT) + 1)
        self.slot = rel % NT
        self.par = rel % 2
        self.chunks = pair * (2 * NT * FC) + rel * FC
        self.first = rel % NT == 0


def tiles_of(pair, tick):
    def t(k, lag):
        rel = 2 * (tick - lag) + k
        if isinstance(pair, int) and not 0 <= pair * (2 * NT) + rel < LAYERS * NT:
            return None
        return Tile(pair, rel)

    def n(k, lag):
        count = pair * (2 * NT) + (2 * (tick - lag) + k + 1)
        return max(0, min(LAYERS * NT, count)) if isinstance(pair, int) else count
    return t, n


def at_least(eng, sem, value):
    if not isinstance(value, int) or value > 0:
        eng.wait_ge(sem, value)


def bank_left(eng, sem, value, other=None, other_value=0):
    if other is None or isinstance(other_value, int):
        at_least(eng, sem, value)
    if other is not None:
        at_least(eng, other, other_value)


def wait_apart(eng, s, sem, value):
    if not isinstance(value, int):
        value = eng.to_reg(value)
        eng.wait_ge(s.consts, 1)
    eng.wait_ge(sem, value)


def column(m, base, layer, k=0, per=1):
    if isinstance(layer, int):
        c = base + layer * per + k
        return m.par[:, c:c + 1]
    return m.par[:, bass.ds(layer * per + (base + k), 1)]


def macaron(nc, x_in, Wq, bq, Wk, bk, Wv, bv, Wo, bo, ln1_s, ln1_b, W1, b1, W2, b2, ln2_s, ln2_b,
            w_up, w_down, ident_in, out):
    x_rows = x_in.rearrange("b s d -> (b s) d").rearrange("(t j p) d -> t p j d", j=BLK, p=P)
    out_rows = out.rearrange("b s d -> (b s) d").rearrange("(t j p) d -> t p j d", j=BLK, p=P)
    W2_rows = W2.rearrange("l (c p) d -> l p c d", p=P)

    with ExitStack() as ctx:
        m, s = Shared(), Shared()

        def sb(name, shape, dt=F32):
            return ctx.enter_context(nc.sbuf_tensor(name, [P] + shape, dt))

        def sem(name):
            return ctx.enter_context(nc.semaphore(name))

        bank = [ctx.enter_context(nc.psum_tensor(f"bank{i}", [P, TILE], F32)) for i in range(8)]
        m.ps_q, m.ps_k, m.ps_v, m.ps_o, m.ps_h0, m.ps_h1, m.ps_ty, m.ps_tz = bank
        m.ps_h = (m.ps_h0, m.ps_h1)
        m.ps_turn = (m.ps_ty, m.ps_tz)

        m.ident = sb("ident", [P])
        m.ones = sb("ones", [P])
        m.eps = sb("eps", [1])
        m.minus_half = sb("minus_half", [BLK])
        m.plus_half = sb("plus_half", [BLK])
        m.x_tm = sb("x_tm", [NT, BLK, P])
        m.x_fm = sb("x_fm", [NT, TILE])
        m.x_hi = sb("x_hi", [NT, TILE], F32R)
        m.x_lo = sb("x_lo", [NT, TILE], F32R)
        m.par_rows = sb("par_rows", [P])
        m.par = sb("par", [NPAR + 2 * LAYERS])
        m.upT = sb("upT", [FC, P], F32R)
        m.downT = sb("downT", [FC, P])
        m.wqkv = [[sb(f"wqkv{i}_{x}", [3, P], F32R) for x in ("hi", "lo")] for i in range(2)]
        m.w1 = [[sb(f"w1{i}_{x}", [FC, P], F32R) for x in ("hi", "lo")] for i in range(2)]
        m.wo = [sb(f"wo{i}", [P]) for i in range(2)]
        m.w2 = [sb(f"w2{i}", [FC, P]) for i in range(2)]
        m.raw_qkv = sb("raw_qkv", [3, P])
        m.raw_w1 = sb("raw_w1", [FC, P])

        m.e_k = sb("e_k", [2, TILE])
        m.e_q = sb("e_q", [2, TILE])
        m.elu_k = sb("elu_k", [2, TILE])
        m.elu_q = sb("elu_q", [2, TILE])
        m.kf = sb("kf", [2, TILE])
        m.kvf = sb("kvf", [2, TILE])
        m.ksum = sb("ksum", [2, 2])
        m.kvacc = sb("kvacc", [2, 2])
        m.kv = sb("kv", [2, 2])
        m.den = sb("den", [2, TILE])
        m.num = sb("num", [2, TILE])
        m.rec = sb("rec", [2, TILE])
        m.nwt = sb("nwt", [2, TILE])
        m.vf = sb("vf", [2, TILE])
        m.y = [sb(f"y{i}", [2, TILE]) for i in (1, 2)]
        m.z = [sb(f"z{i}", [2, BLK, P]) for i in (1, 2)]
        m.st = [sb(f"st{i}", [2, BLK, 6]) for i in (1, 2)]
        m.mv = [sb(f"mv{i}", [2, BLK, 2]) for i in (1, 2)]
        m.ve = [sb(f"ve{i}", [2, BLK]) for i in (1, 2)]
        m.rstd = [sb(f"rstd{i}", [2, BLK]) for i in (1, 2)]
        m.h = sb("h", [2, FC, TILE])

        s.ternary_loaded = sem("ternary_loaded")
        s.vectors_loaded = sem("vectors_loaded")
        s.consts = sem("consts")
        s.abs_sums = sem("abs_sums")
        s.abs_total = sem("abs_total")
        s.thresholds = sem("thresholds")
        s.above = sem("above")
        s.ternary = sem("ternary")
        s.ternary_turned = sem("ternary_turned")
        s.par_turned = sem("par_turned")
        s.ternary_kept = sem("ternary_kept")
        s.par_kept = sem("par_kept")
        s.par_ready = sem("par_ready")
        s.raw_qkv_loaded = sem("raw_qkv_loaded")
        s.raw_w1_loaded = sem("raw_w1_loaded")
        s.wo_loaded = [sem(f"wo{i}_loaded") for i in range(2)]
        s.w2_loaded = [sem(f"w2{i}_loaded") for i in range(2)]
        s.raw_qkv_hi = sem("raw_qkv_hi")
        s.raw_w1_hi = sem("raw_w1_hi")
        s.qkv_split = sem("qkv_split")
        s.w1_split = sem("w1_split")
        s.proj_k = sem("proj_k")
        s.proj_q = sem("proj_q")
        s.proj_v = sem("proj_v")
        s.proj_o = sem("proj_o")
        s.ff_up = sem("ff_up")
        s.ff_down = sem("ff_down")
        s.turned_y1 = sem("turned_y1")
        s.turned_z1 = sem("turned_z1")
        s.turned_y2 = sem("turned_y2")
        s.turned_z2 = sem("turned_z2")
        s.exp_k = sem("exp_k")
        s.exp_q = sem("exp_q")
        s.ksum = sem("ksum")
        s.log_den = sem("log_den")
        s.recip = sem("recip")
        s.gelu_o = sem("gelu_o")
        s.gelu_h = sem("gelu_h")
        s.gelu_ff = sem("gelu_ff")
        s.x1_full = sem("x1_full")
        s.x_full = sem("x_full")
        s.neg_k = sem("neg_k")
        s.neg_q = sem("neg_q")
        s.expm1_k = sem("expm1_k")
        s.expm1_q = sem("expm1_q")
        s.elu_k = sem("elu_k")
        s.elu_q = sem("elu_q")
        s.kv_acc = sem("kv_acc")
        s.kv_ready = sem("kv_ready")
        s.newton_a = sem("newton_a")
        s.newton_c = sem("newton_c")
        s.v_ready = sem("v_ready")
        s.stats1 = sem("stats1")
        s.mv1 = sem("mv1")
        s.z1 = sem("z1")
        s.x1_hi = sem("x1_hi")
        s.stats2 = sem("stats2")
        s.mv2 = sem("mv2")
        s.z2 = sem("z2")
        s.x_hi = sem("x_hi")
        s.den_ready = sem("den_ready")
        s.num_ready = sem("num_ready")
        s.y1 = sem("y1")
        s.y2 = sem("y2")
        s.ve1 = sem("ve1")
        s.ve2 = sem("ve2")
        s.rstd1 = sem("rstd1")
        s.rstd2 = sem("rstd2")
        s.x1_split = sem("x1_split")
        s.x_split = sem("x_split")

        f = [ffn_buffers(sb, sem, m, tag) for tag in ("in", "out")]
        d = Shared()
        d.x_rows, d.out_rows, d.ident, d.w_up, d.w_down = x_rows, out_rows, ident_in, w_up, w_down
        d.kqv, d.Wo, d.W1, d.W2, d.b1 = (Wk, Wq, Wv), Wo, W1, W2_rows, b1
        d.vectors = ((BQ, bq), (BK, bk), (BV, bv), (BO, bo), (LN1S, ln1_s), (LN1B, ln1_b), (B2, b2),
                     (LN2S, ln2_s), (LN2B, ln2_b))

        block = ctx.enter_context(nc.Block())

        @block.sync
        def _(sp):
            sync_engine(sp, m, s, f, d)

        @block.tensor
        def _(pe):
            tensor_engine(pe, m, s, f)

        @block.scalar
        def _(act):
            scalar_engine(act, m, s, f)

        @block.vector
        def _(dve):
            vector_engine(dve, m, s, f)

        @block.gpsimd
        def _(pool):
            gpsimd_engine(pool, m, s, f)


def ffn_buffers(sb, sem, m, tag):
    f = Shared()
    f.first = tag == "in"
    if f.first:
        m.zc = [sb(f"zc_{x}", [2, TILE], F32R) for x in ("hi", "lo")]
        m.hsq = sb("hsq", [2, FC, TILE])
        m.hss = sb("hss", [2, TILE])
        m.scale = sb("scale", [2, 8, BLK])
        m.fz = sb("fz", [2, BLK, P])
        m.fst = sb("fst", [2, BLK, 6])
        m.fmv = sb("fmv", [2, BLK, 2])
        m.raw_tern, m.tern, m.below = m.hsq[:, 1, 0:2, :], m.hsq[:, 0, 0:2, :], m.hsq[:, 0, 2:4, :]
        m.abs_row = sb("abs_row", [2])
        m.thr = sb("thr", [2, 2])
    f.loaded = [sem(f"ffn_{tag}_loaded_{t}") for t in range(NT if f.first else 0)]
    f.stored = sem(f"ffn_{tag}_stored")
    f.turned_x = sem(f"ffn_{tag}_turned_x")
    f.x_in = sem(f"ffn_{tag}_x_in")
    f.stats = sem(f"ffn_{tag}_stats")
    f.mv = sem(f"ffn_{tag}_mv")
    f.var_eps = sem(f"ffn_{tag}_var_eps")
    f.rstd = sem(f"ffn_{tag}_rstd")
    f.sd = sem(f"ffn_{tag}_sd")
    f.sd_rstd = sem(f"ffn_{tag}_sd_rstd")
    f.den = sem(f"ffn_{tag}_den")
    f.part_sums = sem(f"ffn_{tag}_part_sums")
    f.recip = sem(f"ffn_{tag}_recip")
    f.alpha = sem(f"ffn_{tag}_alpha")
    f.z = sem(f"ffn_{tag}_z")
    f.turned_z = sem(f"ffn_{tag}_turned_z")
    f.z_hi = sem(f"ffn_{tag}_z_hi")
    f.z_lo = sem(f"ffn_{tag}_z_lo")
    f.up = sem(f"ffn_{tag}_up")
    f.gelu = sem(f"ffn_{tag}_gelu")
    f.hsq = sem(f"ffn_{tag}_hsq")
    f.hss = sem(f"ffn_{tag}_hss")
    f.ssq = sem(f"ffn_{tag}_ssq")
    f.down = sem(f"ffn_{tag}_down")
    f.ms = sem(f"ffn_{tag}_ms")
    f.rms = sem(f"ffn_{tag}_rms")
    f.rms_eps = sem(f"ffn_{tag}_rms_eps")
    f.rms_recip = sem(f"ffn_{tag}_rms_recip")
    f.beta = sem(f"ffn_{tag}_beta")
    f.x_new = sem(f"ffn_{tag}_x_new")
    f.stats_c = sem(f"ffn_{tag}_stats_c")
    f.mv_c = sem(f"ffn_{tag}_mv_c")
    f.ve_c = sem(f"ffn_{tag}_ve_c")
    f.rstd_c = sem(f"ffn_{tag}_rstd_c")
    f.z_c = sem(f"ffn_{tag}_z_c")
    f.turned_c = sem(f"ffn_{tag}_turned_c")
    return f



def sync_engine(sp, m, s, f, d):
    fin, fout = f
    sp.dma_start(m.raw_tern[:, 0, :].rearrange("p (c d) -> p c d", c=FC),
                 d.w_up.rearrange("(c p) d -> p c d", p=P)).then_inc(s.ternary_loaded, DMA)
    sp.dma_start(m.raw_tern[:, 1, :], d.w_down).then_inc(s.ternary_loaded, DMA)
    sp.dma_start(m.ident[:, :], d.ident).then_inc(s.ternary_loaded, DMA)
    sp.dma_start(m.x_tm[:, 0, :, :], d.x_rows[0]).then_inc(fin.loaded[0], DMA)

    def load_qkv(layer):
        for k, w in enumerate(d.kqv):
            sp.dma_start(m.raw_qkv[:, k, :],
                         w[bass.ds(layer, 1)].rearrange("l p d -> p (l d)")).then_inc(s.raw_qkv_loaded, DMA)

    def load_w1(layer):
        sp.dma_start(m.raw_w1[:, :, :].rearrange("p c d -> p (c d)"),
                     d.W1[bass.ds(layer, 1)].rearrange("l p d -> p (l d)")).then_inc(s.raw_w1_loaded, DMA)

    load_qkv(0)
    sp.dma_start(m.x_tm[:, 1, :, :], d.x_rows[1]).then_inc(fin.loaded[1], DMA)
    for base, v in d.vectors:
        sp.dma_start(m.par_rows[base:base + LAYERS, :], v).then_inc(s.vectors_loaded, DMA)
    sp.dma_start(m.par_rows[B1:NPAR, :], d.b1.rearrange("l (c p) -> (l c) p", p=P)).then_inc(s.vectors_loaded, DMA)
    for t in range(2, NT):
        sp.dma_start(m.x_tm[:, t, :, :], d.x_rows[t]).then_inc(fin.loaded[t], DMA)
    load_w1(0)

    def load_weights(pair, i):
        layer = pair * 2 + i
        row = bass.ds(layer, 1)
        if not isinstance(layer, int) or layer > 0:
            wait_apart(sp, s, s.qkv_split, layer)
            load_qkv(layer)
            wait_apart(sp, s, s.w1_split, layer)
            load_w1(layer)
        if not isinstance(pair, int):
            wait_apart(sp, s, s.proj_o, layer * NT - NT)
        sp.dma_start(m.wo[i][:, :], d.Wo[row].rearrange("l p d -> p (l d)")).then_inc(s.wo_loaded[i], DMA)
        if not isinstance(pair, int):
            wait_apart(sp, s, s.ff_down, layer * NT - NT)
        sp.dma_start(m.w2[i][:, :, :], d.W2[row].rearrange("l p c d -> p (l c) d")).then_inc(s.w2_loaded[i], DMA)

    load_weights(0, 0)
    load_weights(0, 1)
    with sp.Fori(1, PAIRS) as pair:
        load_weights(pair, 0)
        load_weights(pair, 1)
    with sp.Fori(0, NT) as t:
        wait_apart(sp, s, fout.x_new, t + 1)
        sp.dma_start(d.out_rows[bass.ds(t, 1)].rearrange("t p j d -> p (t j) d"),
                     m.x_tm[:, bass.ds(t, 1), :, :].rearrange("p t j d -> p (t j) d")).then_inc(fout.stored, DMA)
    sp.wait_ge(fout.stored, DMA * NT)



def transpose_tile(pe, bank, src, m):
    for j in range(BLK):
        last = pe.transpose(bank[:, j * P:(j + 1) * P], src(j), m.ident[:, :])
    return last


def split_product(pe, bank, w_hi, w_lo, x_hi, x_lo):
    pe.matmul(bank[:, :], w_hi, x_hi, start=True, stop=False)
    pe.matmul(bank[:, :], w_hi, x_lo, start=False, stop=False)
    return pe.matmul(bank[:, :], w_lo, x_hi, start=False, stop=True)


def tensor_engine(pe, m, s, f):
    pe.wait_ge(s.consts, 1)
    pe.wait_ge(s.abs_sums, 2)
    pe.matmul(m.ps_k[:, 0:2], m.ones[:, :], m.abs_row[:, :], start=True, stop=True).then_inc(s.abs_total, 1)
    pe.wait_ge(s.ternary_loaded, DMA * 3)
    for w, dst in ((0, m.ps_v), (1, m.ps_o)):
        pe.wait_ge(s.ternary, w + 1)
        for c in range(FC):
            last = pe.transpose(dst[:, c * P:(c + 1) * P], m.tern[:, w, c * P:(c + 1) * P], m.ident[:, :])
        last.then_inc(s.ternary_turned, 1)
    pe.wait_ge(s.vectors_loaded, DMA * 10)
    pe.wait_ge(s.thresholds, 2)
    pe.transpose(m.ps_k[:, 0:NPAR], m.par_rows[0:NPAR, :], m.ident[0:NPAR, 0:NPAR]).then_inc(s.par_turned, 1)
    pe.wait_ge(s.ternary_kept, 2)

    tensor_ffn(pe, m, s, f[0])
    for tick in range(2 * TICKS):
        tensor_tick(pe, m, s, f, 0, tick)
    with pe.Fori(1, PAIRS) as pair:
        for tick in range(2 * TICKS):
            tensor_tick(pe, m, s, f, pair, tick)
    for tick in range(LAG):
        tensor_tick(pe, m, s, f, PAIRS, tick)
    tensor_ffn(pe, m, s, f[1])


def tensor_tick(pe, m, s, f, pair, tick):
    t, n = tiles_of(pair, tick)

    def project(T, i):
        if not T:
            return
        if T.first:
            pe.wait_ge(s.qkv_split, T.layer + 1)
            if isinstance(T.n, int) and T.n == 1:
                pe.wait_ge(s.par_ready, 1)
                pe.wait_ge(f[0].x_new, NT)
                pe.wait_ge(f[0].ms, NT)
        pe.wait_ge(s.x_split, T.n)
        bank, read, done = ((m.ps_k, s.elu_k, s.proj_k), (m.ps_q, s.elu_q, s.proj_q), (m.ps_v, s.kv_acc, s.proj_v))[i]
        at_least(pe, read, T.n - 1)
        w_hi, w_lo = m.wqkv[T.weights]
        split_product(pe, bank, w_hi[:, i, :], w_lo[:, i, :], m.x_hi[:, T.slot, :], m.x_lo[:, T.slot, :]).then_inc(done, 1)

    def project_o(T, *before):
        if not T:
            return
        if T.first:
            pe.wait_ge(s.wo_loaded[T.weights], T.loads * DMA)
        pe.wait_ge(s.v_ready, T.n)
        bank_left(pe, s.gelu_o, T.n - 1, *before)
        pe.matmul(m.ps_o[:, :], m.wo[T.weights][:, :], m.vf[:, T.par, :], start=True, stop=True).then_inc(s.proj_o, 1)

    def up(T, c):
        if not T:
            return
        if c == 0:
            if T.first:
                pe.wait_ge(s.w1_split, T.layer + 1)
            pe.wait_ge(s.x1_split, T.n)
        at_least(pe, s.gelu_h, T.chunks + (c - 1))
        w_hi, w_lo = m.w1[T.weights]
        split_product(pe, m.ps_h[c % 2], w_hi[:, c, :], w_lo[:, c, :],
                      m.x_hi[:, T.slot, :], m.x_lo[:, T.slot, :]).then_inc(s.ff_up, 1)

    def down(T, c, *before):
        if not T:
            return
        if c == 0:
            if T.first:
                pe.wait_ge(s.w2_loaded[T.weights], T.loads * DMA)
            bank_left(pe, s.gelu_ff, T.n - 1, *before)
        pe.wait_ge(s.gelu_h, T.chunks + (c + 1))
        mm = pe.matmul(m.ps_o[:, :], m.w2[T.weights][:, c, :], m.h[:, T.par, c, :], start=c == 0, stop=c == FC - 1)
        if c == FC - 1:
            mm.then_inc(s.ff_down, 1)

    def turn_y(T, i, *before):
        if not T:
            return
        pe.wait_ge((s.y1, s.y2)[i], T.n)
        bank_left(pe, (s.z1, s.z2)[i], T.n - 1, *before)
        y = m.y[i][:, T.par, :]
        transpose_tile(pe, m.ps_turn[i], lambda j: y[:, j * P:(j + 1) * P], m).then_inc((s.turned_y1, s.turned_y2)[i], 1)

    def turn_z(T, i, *before):
        if not T:
            return
        pe.wait_ge((s.z1, s.z2)[i], T.n)
        bank_left(pe, (s.x1_full, s.x_full)[i], T.n - 1 + (0, NT)[i], *before)
        transpose_tile(pe, m.ps_turn[1 - i], lambda j: m.z[i][:, T.par, j, :], m).then_inc((s.turned_z1, s.turned_z2)[i], 1)

    turn_z(t(1, 3), 0, s.z2, n(0, 4))
    turn_z(t(0, 4), 1, s.z1, n(1, 3))
    project_o(t(0, 2), s.gelu_ff, n(1, 4))
    up(t(0, 3), 2)
    turn_y(t(1, 4), 1, s.x1_full, n(1, 3))
    project_o(t(1, 2))
    up(t(0, 3), 3)
    turn_y(t(0, 2), 0, s.x_full, n(0, 4) + NT)
    down(t(0, 3), 0, s.gelu_o, n(1, 2))
    down(t(0, 3), 1)
    up(t(1, 3), 0)
    up(t(1, 3), 1)
    down(t(0, 3), 2)
    down(t(0, 3), 3)
    project(t(0, 0), KEY)
    turn_z(t(1, 4), 1, s.z1, n(0, 2))
    turn_z(t(0, 2), 0, s.z2, n(1, 4))
    project(t(0, 0), QUERY)
    up(t(1, 3), 2)
    up(t(1, 3), 3)
    turn_y(t(0, 3), 1, s.x1_full, n(0, 2))
    turn_y(t(1, 2), 0, s.x_full, n(1, 4) + NT)
    project(t(0, 0), VALUE)
    down(t(1, 3), 0)
    down(t(1, 3), 1)
    up(t(0, 2), 0)
    up(t(0, 2), 1)
    project(t(1, 0), QUERY)
    project(t(1, 0), KEY)
    down(t(1, 3), 2)
    down(t(1, 3), 3)
    project(t(1, 0), VALUE)


def tensor_ffn(pe, m, s, f):
    ps_down = (m.ps_q, m.ps_o)

    def enter(t):
        if not 0 <= t < NT:
            return
        pe.wait_ge(s.x_full, LAYERS * NT + t + 1)
        at_least(pe, f.x_in, t)
        transpose_tile(pe, m.ps_k, lambda j: m.x_fm[:, t, j * P:(j + 1) * P], m).then_inc(f.turned_x, 1)

    def turn(t):
        if not 0 <= t < NT:
            return
        pe.wait_ge(f.z, t + 1)
        at_least(pe, f.z_lo, t)
        if t == 0 and not f.first:
            pe.wait_ge(s.x_full, (LAYERS + 1) * NT)
            pe.wait_ge(s.gelu_h, LAYERS * NT * FC)
        transpose_tile(pe, m.ps_ty, lambda j: m.fz[:, t % 2, j, :], m).then_inc(f.turned_z, 1)

    def up(t, c):
        if not 0 <= t < NT:
            return
        if c == 0:
            pe.wait_ge(f.z_lo, t + 1)
        at_least(pe, f.gelu, FC * t + c - 1)
        pe.matmul(m.ps_h[c % 2][:, :], m.upT[:, c, :], m.zc[0][:, t % 2, :], start=True, stop=False)
        pe.matmul(m.ps_h[c % 2][:, :], m.upT[:, c, :], m.zc[1][:, t % 2, :], start=False, stop=True).then_inc(f.up, 1)

    def down(t):
        if not 0 <= t < NT:
            return
        at_least(pe, f.x_new, t - 1)
        if t == 0 and not f.first:
            pe.wait_ge(s.gelu_ff, LAYERS * NT)
            pe.wait_ge(s.elu_q, LAYERS * NT)
        pe.wait_ge(f.gelu, FC * (t + 1))
        for j in range(BLK):
            for c in range(FC):
                last = pe.matmul(ps_down[t % 2][:, j * P:(j + 1) * P], m.h[:, t % 2, c, j * P:(j + 1) * P],
                                 m.downT[:, c, :], start=c == 0, stop=c == FC - 1)
        last.then_inc(f.down, 1)

    def squares(t):
        if not 0 <= t < NT:
            return
        pe.wait_ge(f.hss, t + 1)
        at_least(pe, f.ms, t)
        for j in range(BLK):
            last = pe.matmul(m.ps_v[:, j:j + 1], m.hss[:, t % 2, j * P:(j + 1) * P], m.ones[:, 0:1],
                             start=True, stop=True)
        last.then_inc(f.ssq, 1)

    def turn_c(t):
        if not 0 <= t < NT:
            return
        pe.wait_ge(f.z_c, t + 1)
        at_least(pe, s.x_hi, t)
        transpose_tile(pe, m.ps_tz, lambda j: m.z[0][:, t % 2, j, :], m).then_inc(f.turned_c, 1)

    for tick in range(NT + (10 if f.first else 6)):
        if f.first:
            up(tick - 1, 0)
            up(tick - 1, 1)
            turn(tick - 0)
            squares(tick - 3)
            up(tick - 1, 2)
            up(tick - 1, 3)
            turn_c(tick - 7)
            down(tick - 2)
        else:
            up(tick - 5, 2)
            turn(tick - 4)
            up(tick - 5, 3)
            down(tick - 6)
            up(tick - 4, 0)
            up(tick - 4, 1)
            squares(tick - 6)
            enter(tick - 0)



def scalar_engine(act, m, s, f):
    scalar_ffn(act, m, s, f[0])
    for tick in range(2 * TICKS):
        scalar_tick(act, m, s, 0, tick)
    with act.Fori(1, PAIRS) as pair:
        for tick in range(2 * TICKS):
            scalar_tick(act, m, s, pair, tick)
    for tick in range(LAG):
        scalar_tick(act, m, s, PAIRS, tick)
    scalar_ffn(act, m, s, f[1])


def scalar_tick(act, m, s, pair, tick):
    t, n = tiles_of(pair, tick)

    def negative(T, i):
        if not T:
            return
        e, bank, base, proj, done = ((m.e_k, m.ps_k, NEG_BK, s.proj_k, s.neg_k), (m.e_q, m.ps_q, NEG_BQ, s.proj_q, s.neg_q))[i]
        wait_apart(act, s, proj, T.n)
        act.activation(e[:, T.par, :], bank[:, :], ACT.Relu, bias=column(m, base, T.layer), scale=-1.0).then_inc(done, 1)

    def exp(T, i):
        if not T:
            return
        e, neg, done = ((m.e_k, s.neg_k, s.exp_k), (m.e_q, s.neg_q, s.exp_q))[i]
        wait_apart(act, s, neg, T.n)
        act.activation(e[:, T.par, :], e[:, T.par, :], ACT.Exp, scale=-1.0).then_inc(done, 1)

    def sum_k(T):
        if not T:
            return
        wait_apart(act, s, s.elu_k, T.n)
        for b in range(2):
            cols = slice(b * SEQ, (b + 1) * SEQ)
            last = act.activation(m.kf[:, T.par, cols], m.elu_k[:, T.par, cols], ACT.Identity, bias=1.0,
                                  accum_out=m.ksum[:, T.par, b:b + 1])
        last.then_inc(s.ksum, 1)

    def log_den(T):
        if not T:
            return
        wait_apart(act, s, s.den_ready, T.n)
        act.activation(m.rec[:, T.par, :], m.den[:, T.par, :], ACT.Ln, bias=m.eps[:, 0:1]).then_inc(s.log_den, 1)

    def recip(T):
        if not T:
            return
        wait_apart(act, s, s.log_den, T.n)
        act.activation(m.rec[:, T.par, :], m.rec[:, T.par, :], ACT.Exp, scale=-1.0).then_inc(s.recip, 1)

    def gelu(bank, ready, n, dst, bias, done):
        wait_apart(act, s, ready, n)
        act.activation(dst, bank[:, :], ACT.Gelu_apprx_tanh, bias=bias).then_inc(done, 1)

    def gelu_o(T):
        if T:
            gelu(m.ps_o, s.proj_o, T.n, m.y[0][:, T.par, :], column(m, BO, T.layer), s.gelu_o)

    def gelu_h(T, c):
        if T:
            gelu(m.ps_h[c % 2], s.ff_up, T.chunks + (c + 1), m.h[:, T.par, c, :],
                 column(m, B1, T.layer, c, FC), s.gelu_h)

    def gelu_ff(T):
        if T:
            gelu(m.ps_o, s.ff_down, T.n, m.y[1][:, T.par, :], column(m, B2, T.layer), s.gelu_ff)

    def full(T, i):
        if not T:
            return
        wait_apart(act, s, (s.turned_z1, s.turned_z2)[i], T.n)
        act.activation(m.x_fm[:, T.slot, :], m.ps_turn[1 - i][:, :], ACT.Identity,
                       bias=column(m, (LN1B, LN2B)[i], T.layer),
                       scale=column(m, (LN1S, LN2S)[i], T.layer)).then_inc((s.x1_full, s.x_full)[i], 1)

    act.preload_act_table_set(EXP_AND_LN)
    exp(t(0, 1), QUERY)
    exp(t(0, 1), KEY)
    log_den(t(0, 2))
    recip(t(0, 2))
    log_den(t(1, 2))
    recip(t(1, 2))
    negative(t(1, 1), QUERY)
    negative(t(1, 1), KEY)
    exp(t(1, 1), QUERY)
    exp(t(1, 1), KEY)
    gelu_ff(t(1, 4))
    gelu_h(t(0, 3), 0)
    full(t(1, 3), 0)
    gelu_o(t(0, 2))
    gelu_h(t(0, 3), 1)
    full(t(0, 4), 1)
    gelu_o(t(1, 2))
    sum_k(t(0, 1))
    gelu_h(t(0, 3), 2)
    gelu_h(t(0, 3), 3)
    sum_k(t(1, 1))
    gelu_h(t(1, 3), 0)
    gelu_h(t(1, 3), 1)
    gelu_ff(t(0, 3))
    negative(t(0, 0), KEY)
    full(t(1, 4), 1)
    full(t(0, 2), 0)
    negative(t(0, 0), QUERY)
    gelu_h(t(1, 3), 2)
    gelu_h(t(1, 3), 3)


def scalar_ffn(act, m, s, f):
    def z_hi(t):
        if not 0 <= t < NT:
            return
        act.wait_ge(f.turned_z, t + 1)
        at_least(act, f.up, FC * (t - 1))
        act.activation(m.zc[0][:, t % 2, :], m.ps_ty[:, :], ACT.Copy).then_inc(f.z_hi, 1)

    def gelu(t, c):
        if not 0 <= t < NT:
            return
        act.wait_ge(f.up, FC * t + c + 1)
        if c == 0:
            at_least(act, f.down, t - 1)
        act.activation(m.h[:, t % 2, c, :], m.ps_h[c % 2][:, :], ACT.Gelu).then_inc(f.gelu, 1)

    def square(t):
        if not 0 <= t < NT:
            return
        act.wait_ge(f.gelu, FC * (t + 1))
        at_least(act, f.hss, t - 1)
        act.activation(m.hsq[:, t % 2, :, :], m.h[:, t % 2, :, :], ACT.Square).then_inc(f.hsq, 1)

    def full(t):
        if not 0 <= t < NT:
            return
        act.wait_ge(f.turned_c, t + 1)
        act.activation(m.x_fm[:, t, :], m.ps_tz[:, :], ACT.Copy).then_inc(s.x_full, 1)

    def hi(t):
        if not 0 <= t < NT:
            return
        act.wait_ge(f.turned_c, t + 1)
        act.activation(m.x_hi[:, t, :], m.ps_tz[:, :], ACT.Copy).then_inc(s.x_hi, 1)

    for tick in range(NT + (10 if f.first else 6)):
        if f.first:
            gelu(tick - 2, 2)
            gelu(tick - 2, 3)
            square(tick - 2)
            gelu(tick - 1, 0)
            gelu(tick - 1, 1)
            z_hi(tick - 0)
            full(tick - 8)
            hi(tick - 8)
        else:
            square(tick - 2)
            gelu(tick - 1, 0)
            gelu(tick - 1, 1)
            gelu(tick - 1, 2)
            z_hi(tick - 0)
            gelu(tick - 1, 3)



def block_stats(dve, src, st, done):
    for j in range(BLK):
        last = dve.bn_stats(st[:, j, :], src(j))
    last.then_inc(done, 1)


def block_means(dve, s, st, mv, ready, n, done):
    wait_apart(dve, s, ready, n)
    for j in range(BLK):
        last = dve.bn_aggr(mv[:, j, :], st[:, j, :])
    last.then_inc(done, 1)


def normalise(dve, dst, src, mv, scale, done):
    for j in range(BLK):
        last = dve.tensor_scalar(dst[:, j, :], src(j), mv[:, j, 0:1], scale[:, j:j + 1], ALU.subtract, ALU.mult)
    last.then_inc(done, 1)


def vector_engine(dve, m, s, f):
    dve.wait_ge(s.ternary_loaded, DMA * 3)
    for w in range(2):
        dve.tensor_reduce(m.abs_row[:, w:w + 1], m.raw_tern[:, w, :], AX_X, ALU.add,
                          apply_absolute_value=True).then_inc(s.abs_sums, 1)
    dve.wait_ge(s.abs_total, 1)
    for i, half in enumerate((0.5, -0.5)):
        dve.tensor_scalar(m.thr[:, i, :], m.ps_k[:, 0:2], 1.0 / (FF * P), half, ALU.mult,
                          ALU.mult).then_inc(s.thresholds, 1)
    dve.wait_ge(s.thresholds, 2)
    for w in range(2):
        dve.tensor_scalar(m.below[:, w, :], m.raw_tern[:, w, :], m.thr[:, 1, w:w + 1], None,
                          ALU.is_lt).then_inc(s.above, 1)
    for w in range(2):
        dve.wait_ge(s.above, w + 1)
        dve.scalar_tensor_tensor(m.tern[:, w, :], m.raw_tern[:, w, :], m.thr[:, 0, w:w + 1], m.below[:, w, :],
                                 ALU.is_gt, ALU.subtract).then_inc(s.ternary, 1)
    for w, dst, bank in ((0, m.upT, m.ps_v), (1, m.downT, m.ps_o)):
        dve.wait_ge(s.ternary_turned, w + 1)
        dve.tensor_copy(dst[:, :, :].rearrange("p c d -> p (c d)"), bank[:, :]).then_inc(s.ternary_kept, 1)

    vector_ffn(dve, m, s, f[0])
    dve.wait_ge(s.par_turned, 1)
    dve.tensor_copy(m.par[:, 0:NPAR], m.ps_k[:, 0:NPAR]).then_inc(s.par_kept, 1)
    dve.wait_ge(s.par_kept, 1)
    dve.tensor_scalar(m.par[:, NEG_BQ:NEG_BK + LAYERS], m.par[:, BQ:BK + LAYERS], -1.0, None,
                      ALU.mult).then_inc(s.par_ready, 1)
    for tick in range(2 * TICKS):
        vector_tick(dve, m, s, 0, tick)
    with dve.Fori(1, PAIRS) as pair:
        for tick in range(2 * TICKS):
            vector_tick(dve, m, s, pair, tick)
    for tick in range(LAG):
        vector_tick(dve, m, s, PAIRS, tick)
    vector_ffn(dve, m, s, f[1])


def vector_tick(dve, m, s, pair, tick):
    t, n = tiles_of(pair, tick)

    def minus_one(T, i):
        if not T:
            return
        e, exp, done = ((m.e_k, s.exp_k, s.expm1_k), (m.e_q, s.exp_q, s.expm1_q))[i]
        dve.wait_ge(exp, T.n)
        dve.tensor_scalar(e[:, T.par, :], e[:, T.par, :], 1.0, None, ALU.subtract).then_inc(done, 1)

    def elu(T, i):
        if not T:
            return
        e, bank, dst, base, expm1, done = ((m.e_k, m.ps_k, m.elu_k, BK, s.expm1_k, s.elu_k),
                                           (m.e_q, m.ps_q, m.elu_q, BQ, s.expm1_q, s.elu_q))[i]
        if i == QUERY:
            at_least(dve, s.num_ready, T.n - 2)
        dve.wait_ge(expm1, T.n)
        dve.scalar_tensor_tensor(dst[:, T.par, :], bank[:, :], column(m, base, T.layer), e[:, T.par, :],
                                 ALU.add, ALU.max).then_inc(done, 1)

    def sum_kv(T):
        if not T:
            return
        dve.wait_ge(s.elu_k, T.n)
        dve.wait_ge(s.proj_v, T.n)
        for b in range(2):
            cols = slice(b * SEQ, (b + 1) * SEQ)
            last = dve.scalar_tensor_tensor(m.kvf[:, T.par, cols], m.elu_k[:, T.par, cols], 1.0, m.ps_v[:, cols],
                                            ALU.add, ALU.mult, accum_out=m.kvacc[:, T.par, b:b + 1])
        last.then_inc(s.kv_acc, 1)

    def kv(T):
        if not T:
            return
        dve.wait_ge(s.ksum, T.n)
        dve.wait_ge(s.kv_acc, T.n)
        dve.scalar_tensor_tensor(m.kv[:, T.par, :], m.ksum[:, T.par, :], column(m, BV, T.layer),
                                 m.kvacc[:, T.par, :], ALU.mult, ALU.add).then_inc(s.kv_ready, 1)

    def newton_a(T):
        if not T:
            return
        dve.wait_ge(s.recip, T.n)
        dve.scalar_tensor_tensor(m.nwt[:, T.par, :], m.den[:, T.par, :], EPS_ATTN, m.rec[:, T.par, :],
                                 ALU.add, ALU.mult).then_inc(s.newton_a, 1)

    def newton_c(T):
        if not T:
            return
        dve.wait_ge(s.newton_a, T.n)
        dve.scalar_tensor_tensor(m.rec[:, T.par, :], m.nwt[:, T.par, :], 2.0, m.rec[:, T.par, :],
                                 ALU.subtract, ALU.mult).then_inc(s.newton_c, 1)

    def newton_v(T):
        if not T:
            return
        dve.wait_ge(s.num_ready, T.n)
        dve.wait_ge(s.newton_c, T.n)
        dve.scalar_tensor_tensor(m.vf[:, T.par, :], m.num[:, T.par, :], -1.0, m.rec[:, T.par, :],
                                 ALU.mult, ALU.mult).then_inc(s.v_ready, 1)

    def source(i):
        return lambda j: m.ps_turn[i][:, j * P:(j + 1) * P]

    def stats(T, i):
        if not T:
            return
        dve.wait_ge((s.turned_y1, s.turned_y2)[i], T.n)
        block_stats(dve, source(i), m.st[i][:, T.par], (s.stats1, s.stats2)[i])
        block_means(dve, s, m.st[i][:, T.par], m.mv[i][:, T.par], (s.stats1, s.stats2)[i], T.n, (s.mv1, s.mv2)[i])

    def z(T, i):
        if not T:
            return
        dve.wait_ge((s.rstd1, s.rstd2)[i], T.n)
        normalise(dve, m.z[i][:, T.par], source(i), m.mv[i][:, T.par], m.rstd[i][:, T.par], (s.z1, s.z2)[i])

    def hi(T, i):
        if not T:
            return
        full, done, more = ((s.x1_full, s.x1_hi, 0), (s.x_full, s.x_hi, NT))[i]
        dve.wait_ge(full, T.n + more)
        dve.tensor_copy(m.x_hi[:, T.slot, :], m.x_fm[:, T.slot, :]).then_inc(done, 1)

    sum_kv(t(0, 1))
    z(t(1, 3), 0)
    newton_v(t(0, 2))
    newton_a(t(1, 2))
    newton_c(t(1, 2))
    newton_v(t(1, 2))
    hi(t(1, 3), 0)
    minus_one(t(1, 1), QUERY)
    minus_one(t(1, 1), KEY)
    stats(t(1, 4), 1)
    stats(t(0, 2), 0)
    hi(t(0, 4), 1)
    elu(t(1, 1), KEY)
    z(t(1, 4), 1)
    z(t(0, 2), 0)
    elu(t(1, 1), QUERY)
    sum_kv(t(1, 1))
    kv(t(0, 1))
    kv(t(1, 1))
    hi(t(0, 2), 0)
    hi(t(1, 4), 1)
    stats(t(0, 3), 1)
    stats(t(1, 2), 0)
    minus_one(t(0, 0), QUERY)
    minus_one(t(0, 0), KEY)
    elu(t(0, 0), QUERY)
    elu(t(0, 0), KEY)
    newton_a(t(0, 1))
    z(t(0, 3), 1)
    newton_c(t(0, 1))


def vector_ffn(dve, m, s, f):
    eps_var, rstd, sd, den, recip, alpha, ms, beta = range(8)

    def source(t):
        return lambda j: m.x_tm[:, t, j, :]

    def x_in(t):
        if not 0 <= t < NT:
            return
        dve.wait_ge(f.turned_x, t + 1)
        x = m.x_tm[:, t, :, :].rearrange("p j d -> p (j d)")
        dve.tensor_tensor(x, m.ps_k[:, :], x, ALU.add).then_inc(f.x_in, 1)

    def enter_stats(t):
        if not 0 <= t < NT:
            return
        if f.first:
            dve.wait_ge(f.loaded[t], DMA)
        else:
            dve.wait_ge(f.x_in, t + 1)
        block_stats(dve, source(t), m.fst[:, t % 2], f.stats)
        block_means(dve, s, m.fst[:, t % 2], m.fmv[:, t % 2], f.stats, t + 1, f.mv)
        dve.wait_ge(f.mv, t + 1)
        dve.tensor_scalar(m.scale[:, t % 2, eps_var, :], m.fmv[:, t % 2, :, 1], EPS_OUTER, None,
                          ALU.add).then_inc(f.var_eps, 1)

    def alpha_(t):
        if not 0 <= t < NT:
            return
        sc = m.scale[:, t % 2]
        dve.wait_ge(f.sd, t + 1)
        dve.wait_ge(f.rstd, t + 1)
        dve.tensor_tensor(sc[:, sd, :], sc[:, sd, :], sc[:, rstd, :], ALU.mult).then_inc(f.sd_rstd, 1)
        dve.wait_ge(f.sd_rstd, t + 1)
        dve.tensor_scalar(sc[:, den, :], sc[:, sd, :], EPS_RMS, None, ALU.add).then_inc(f.den, 1)
        dve.wait_ge(f.den, t + 1)
        dve.reciprocal(sc[:, recip, :], sc[:, den, :]).then_inc(f.recip, 1)
        dve.wait_ge(f.recip, t + 1)
        dve.tensor_tensor(sc[:, alpha, :], sc[:, recip, :], sc[:, rstd, :], ALU.mult).then_inc(f.alpha, 1)

    def normal(t):
        if not 0 <= t < NT:
            return
        dve.wait_ge(f.alpha, t + 1)
        at_least(dve, f.turned_z, t - 1)
        normalise(dve, m.fz[:, t % 2], source(t), m.fmv[:, t % 2], m.scale[:, t % 2, alpha, :], f.z)

    def low(t):
        if not 0 <= t < NT:
            return
        dve.wait_ge(f.z_hi, t + 1)
        dve.tensor_tensor(m.zc[1][:, t % 2, :], m.ps_ty[:, :], m.zc[0][:, t % 2, :].bitcast(F32),
                          ALU.subtract).then_inc(f.z_lo, 1)

    def mean_square(t):
        if not 0 <= t < NT:
            return
        dve.wait_ge(f.ssq, t + 1)
        dve.tensor_scalar(m.scale[:, t % 2, ms, :], m.ps_v[:, 0:BLK], 1.0 / FF, None, ALU.mult).then_inc(f.ms, 1)

    def beta_(t):
        if not 0 <= t < NT:
            return
        sc = m.scale[:, t % 2]
        dve.wait_ge(f.rms, t + 1)
        dve.tensor_scalar(sc[:, ms, :], sc[:, ms, :], EPS_RMS, None, ALU.add).then_inc(f.rms_eps, 1)
        dve.wait_ge(f.rms_eps, t + 1)
        dve.reciprocal(sc[:, ms, :], sc[:, ms, :]).then_inc(f.rms_recip, 1)
        dve.wait_ge(f.rms_recip, t + 1)
        dve.tensor_scalar(sc[:, beta, :], sc[:, ms, :], 0.5, None, ALU.mult).then_inc(f.beta, 1)

    def residual(t):
        if not 0 <= t < NT:
            return
        sc = m.scale[:, t % 2]
        dve.wait_ge(f.beta, t + 1)
        dve.wait_ge(f.down, t + 1)
        bank = (m.ps_q, m.ps_o)[t % 2]
        for j in range(BLK):
            last = dve.scalar_tensor_tensor(m.x_tm[:, t, j, :], bank[:, j * P:(j + 1) * P], sc[:, beta, j:j + 1],
                                            m.x_tm[:, t, j, :], ALU.mult, ALU.add)
        last.then_inc(f.x_new, 1)

    def stats_c(t):
        if not 0 <= t < NT:
            return
        dve.wait_ge(f.x_new, t + 1)
        block_stats(dve, source(t), m.st[0][:, t % 2], f.stats_c)
        block_means(dve, s, m.st[0][:, t % 2], m.mv[0][:, t % 2], f.stats_c, t + 1, f.mv_c)
        dve.wait_ge(f.mv_c, t + 1)
        dve.tensor_scalar(m.ve[0][:, t % 2, :], m.mv[0][:, t % 2, :, 1], EPS_OUTER, None, ALU.add).then_inc(f.ve_c, 1)

    def z_c(t):
        if not 0 <= t < NT:
            return
        dve.wait_ge(f.rstd_c, t + 1)
        at_least(dve, f.turned_c, t - 1)
        normalise(dve, m.z[0][:, t % 2], source(t), m.mv[0][:, t % 2], m.rstd[0][:, t % 2], f.z_c)

    for tick in range(NT + (10 if f.first else 6)):
        if f.first:
            enter_stats(tick - 0)
            residual(tick - 6)
            low(tick - 2)
            alpha_(tick - 1)
            mean_square(tick - 5)
            stats_c(tick - 6)
            normal(tick - 1)
            beta_(tick - 5)
            z_c(tick - 7)
        else:
            mean_square(tick - 6)
            enter_stats(tick - 1)
            beta_(tick - 6)
            low(tick - 3)
            residual(tick - 6)
            alpha_(tick - 2)
            x_in(tick - 0)
            normal(tick - 2)



def gpsimd_engine(pool, m, s, f):
    pool.memset(m.ones[:, :], 1.0)
    pool.memset(m.eps[:, :], EPS_ATTN)
    pool.memset(m.minus_half[:, :], -0.5)
    pool.memset(m.plus_half[:, :], 0.5).then_inc(s.consts, 1)
    pool.wait_ge(s.consts, 1)
    for k in range(3):
        split_qkv(pool, m, s, 0, 0, k)
    gpsimd_ffn(pool, m, s, f[0])
    for k in range(FC - 1):
        split_w1(pool, m, s, 0, 0, k)
    for tick in range(2 * TICKS + POOL_START):
        gpsimd_tick(pool, m, s, 0, tick)
    with pool.Fori(1, PAIRS) as pair:
        for tick in range(POOL_START, 2 * TICKS + POOL_START):
            gpsimd_tick(pool, m, s, pair, tick)
    for tick in range(POOL_START, LAG):
        gpsimd_tick(pool, m, s, PAIRS, tick)
    gpsimd_ffn(pool, m, s, f[1])


def split(pool, s, layer, raw, hi, lo, k, loaded, count, hi_made, hi_count, used, last, done):
    wait_apart(pool, s, loaded, count)
    if not isinstance(layer, int):
        wait_apart(pool, s, used, layer * NT - NT)
    pool.tensor_copy(hi[:, k, :], raw[:, k, :]).then_inc(hi_made, 1)
    wait_apart(pool, s, hi_made, hi_count)
    low = pool.tensor_tensor(lo[:, k, :], raw[:, k, :], hi[:, k, :].bitcast(F32), ALU.subtract)
    if last:
        low.then_inc(done, 1)


def split_qkv(pool, m, s, layer, i, k):
    split(pool, s, layer, m.raw_qkv, *m.wqkv[i], k, s.raw_qkv_loaded, layer * (3 * DMA) + 3 * DMA,
          s.raw_qkv_hi, layer * 3 + (k + 1), s.proj_v, k == 2, s.qkv_split)


def split_w1(pool, m, s, layer, i, k):
    split(pool, s, layer, m.raw_w1, *m.w1[i], k, s.raw_w1_loaded, layer * DMA + DMA,
          s.raw_w1_hi, layer * FC + (k + 1), s.ff_down, k == FC - 1, s.w1_split)


def inverse_root(pool, m, s, dst, tmp, var, eps, ready, n, mid, done):
    wait_apart(pool, s, ready, n)
    pool.tensor_scalar(tmp, var, eps, None, ALU.add).then_inc(mid, 1)
    wait_apart(pool, s, mid, n)
    pool.tensor_tensor(dst, tmp, m.minus_half[:, :], ALU.pow).then_inc(done, 1)


def gpsimd_tick(pool, m, s, pair, tick):
    t, n = tiles_of(pair, tick)

    def add_residual(T, i):
        if not T:
            return
        wait_apart(pool, s, (s.gelu_o, s.gelu_ff)[i], T.n)
        y = m.y[i][:, T.par, :]
        pool.tensor_tensor(y, y, m.x_fm[:, T.slot, :], ALU.add).then_inc((s.y1, s.y2)[i], 1)

    def rstd(T, i):
        if not T:
            return
        inverse_root(pool, m, s, m.rstd[i][:, T.par, :], m.ve[i][:, T.par, :], m.mv[i][:, T.par, :, 1], EPS_LN,
                     (s.mv1, s.mv2)[i], T.n, (s.ve1, s.ve2)[i], (s.rstd1, s.rstd2)[i])

    def low(T, i):
        if not T:
            return
        hi, done, more = ((s.x1_hi, s.x1_split, 0), (s.x_hi, s.x_split, NT))[i]
        wait_apart(pool, s, hi, T.n + more)
        pool.tensor_tensor(m.x_lo[:, T.slot, :], m.x_fm[:, T.slot, :], m.x_hi[:, T.slot, :].bitcast(F32),
                           ALU.subtract).then_inc(done, 1)

    def scaled_q(T, sums, dst, ready, done):
        wait_apart(pool, s, s.elu_q, T.n)
        wait_apart(pool, s, ready, T.n)
        for b in range(2):
            cols = slice(b * SEQ, (b + 1) * SEQ)
            last = pool.tensor_scalar(dst[:, T.par, cols], m.elu_q[:, T.par, cols], 1.0, sums[:, T.par, b:b + 1],
                                      ALU.add, ALU.mult)
        last.then_inc(done, 1)

    def den(T):
        if T:
            scaled_q(T, m.ksum, m.den, s.ksum, s.den_ready)

    def num(T):
        if T:
            scaled_q(T, m.kv, m.num, s.kv_ready, s.num_ready)

    def split_weights(T):
        if not T:
            return
        if T.slot == 0:
            split_w1(pool, m, s, T.layer, T.weights, FC - 1)
        elif T.slot > 1 and not (isinstance(T.layer, int) and T.layer == LAYERS - 1):
            layer, i = T.layer + 1, 1 - T.weights
            if T.slot < 5:
                split_qkv(pool, m, s, layer, i, T.slot - 2)
            else:
                split_w1(pool, m, s, layer, i, T.slot - 5)

    den(t(0, 0))
    add_residual(t(0, 2), 1)
    num(t(0, 0))
    low(t(1, 3), 1)
    den(t(1, 0))
    low(t(0, 1), 0)
    rstd(t(0, 2), 1)
    rstd(t(1, 1), 0)
    split_weights(t(0, 0))
    split_weights(t(1, 0))
    num(t(1, 0))
    add_residual(t(1, 2), 1)
    add_residual(t(0, 0), 0)
    low(t(1, 1), 0)
    rstd(t(1, 2), 1)
    rstd(t(0, 0), 0)
    low(t(0, 2), 1)
    add_residual(t(1, 0), 0)




def gpsimd_ffn(pool, m, s, f):
    eps_var, rstd_, sd_, den, recip, alpha, ms, beta = range(8)

    def rstd(t):
        if not 0 <= t < NT:
            return
        pool.wait_ge(f.var_eps, t + 1)
        at_least(pool, f.alpha, t - 1)
        pool.tensor_tensor(m.scale[:, t % 2, rstd_, :], m.scale[:, t % 2, eps_var, :], m.minus_half[:, :],
                           ALU.pow).then_inc(f.rstd, 1)

    def sd(t):
        if not 0 <= t < NT:
            return
        pool.wait_ge(f.mv, t + 1)
        at_least(pool, f.alpha, t - 1)
        pool.tensor_tensor(m.scale[:, t % 2, sd_, :], m.fmv[:, t % 2, :, 1], m.plus_half[:, :],
                           ALU.pow).then_inc(f.sd, 1)

    def sum_squares(t):
        if not 0 <= t < NT:
            return
        pool.wait_ge(f.hsq, t + 1)
        sq, total = m.hsq[:, t % 2, :, :], m.hss[:, t % 2, :]
        at_least(pool, f.ssq, t - 1)
        pool.tensor_tensor(total, sq[:, 0, :], sq[:, 1, :], ALU.add).then_inc(f.part_sums, 1)
        pool.wait_ge(f.part_sums, 2 * t + 1)
        pool.tensor_tensor(total, total, sq[:, 2, :], ALU.add).then_inc(f.part_sums, 1)
        pool.wait_ge(f.part_sums, 2 * t + 2)
        pool.tensor_tensor(total, total, sq[:, 3, :], ALU.add).then_inc(f.hss, 1)

    def rms(t):
        if not 0 <= t < NT:
            return
        sc = m.scale[:, t % 2]
        pool.wait_ge(f.ms, t + 1)
        pool.tensor_tensor(sc[:, ms, :], sc[:, ms, :], m.plus_half[:, :], ALU.pow).then_inc(f.rms, 1)

    def rstd_c(t):
        if not 0 <= t < NT:
            return
        pool.wait_ge(f.ve_c, t + 1)
        at_least(pool, f.z_c, t - 1)
        pool.tensor_tensor(m.rstd[0][:, t % 2, :], m.ve[0][:, t % 2, :], m.minus_half[:, :],
                           ALU.pow).then_inc(f.rstd_c, 1)

    def x_low(t):
        if not 0 <= t < NT:
            return
        pool.wait_ge(s.x_hi, t + 1)
        pool.wait_ge(s.x_full, t + 1)
        pool.tensor_tensor(m.x_lo[:, t, :], m.x_fm[:, t, :], m.x_hi[:, t, :].bitcast(F32),
                           ALU.subtract).then_inc(s.x_split, 1)

    for tick in range(NT + (10 if f.first else 6)):
        if f.first:
            rstd(tick - 1)
            rstd_c(tick - 7)
            sum_squares(tick - 4)
            rms(tick - 5)
            sd(tick - 0)
            x_low(tick - 10)
        else:
            sd(tick - 1)
            rstd(tick - 0)
            sum_squares(tick - 3)
            rms(tick - 4)


_INS = ["x", "Wq", "bq", "Wk", "bk", "Wv", "bv", "Wo", "bo", "ln1_s", "ln1_b", "W1", "b1", "W2", "b2",
        "ln2_s", "ln2_b"]
_FFN = ["w_up", "w_down"]


def kernel(**inputs):
    import numpy as np
    import concourse.bacc as bacc
    from concourse.bass_utils import run_bass_kernel_spmd

    nc = bacc.Bacc("TRN2", target_bir_lowering=False, num_devices=1)
    given = [(n, inputs[f"L0_attn_{n}"]) for n in _INS] + [(n, inputs[f"L0_ffn_{n}"]) for n in _FFN]
    given.append(("identity", np.eye(P, dtype=np.float32)))
    arrays, args = {}, []
    for name, value in given:
        a = np.ascontiguousarray(value)
        arrays[f"in_{name}"] = a
        args.append(nc.dram_tensor(f"in_{name}", a.shape, mybir.dt.from_np(a.dtype), kind="ExternalInput").ap())
    x = arrays["in_x"]
    args.append(nc.dram_tensor("out_0", x.shape, F32, kind="ExternalOutput").ap())
    macaron(nc, *args)
    return run_bass_kernel_spmd(nc, [arrays], core_ids=[0]).results[0]["out_0"]
```
